# Optimizing a Trainium2 kernel written in Bass

```python
import numpy as np
import jax
import jax.numpy as jnp

def _softmax(x, axis=-1):
    return jax.nn.softmax(x, axis=axis)

def _gelu(x):
    return jax.nn.gelu(x, approximate=True)

def _silu(x):
    return jax.nn.silu(x)

def _sigmoid(x):
    return jax.nn.sigmoid(x)

def _layernorm(x, axis=-1, eps=1e-05):
    m = jnp.mean(x, axis=axis, keepdims=True)
    v = jnp.var(x, axis=axis, keepdims=True)
    return (x - m) / jnp.sqrt(v + eps)

def _scatter_add(tgt, idx, src, axis=0):
    return tgt.at[idx].add(src)

def _segment_sum(src, seg, n):
    return jax.ops.segment_sum(src, seg, n)
kernel_name = 'mk_vit_tower_postln_d2_tok_img1024_r4_1db0fc'

def setup_inputs(seed: int=0):
    np.random.seed(seed)
    _w = jnp.asarray

    def _rec_inputs():
        import jax
        import jax.numpy as jnp
        _rk = jax.random.key(seed)
        x = -0.000125008 + 0.999885 * jax.random.normal(jax.random.fold_in(_rk, 1), (8, 512, 256, 4), jnp.float32)
        return x
    x = _rec_inputs()

    def _L0_tok_setup():
        import jax, jax.numpy as jnp
        import numpy as np
        key = jax.random.key(seed)
        k1, k2, k3 = jax.random.split(key, 3)
        B, H, I, O, Dp1 = (4, 512, 256, 256, 4)
        x = jax.random.normal(k1, (B, H, I, Dp1), dtype=jnp.float32)
        weight = 0.1 * jax.random.normal(k2, (O, Dp1), dtype=jnp.float32)
        weighted_sum = 0.1 * jax.random.normal(k3, (O, I), dtype=jnp.float32)
        return {'x': x, 'weight': weight, 'weighted_sum': weighted_sum}
    _L0_tok_all = _L0_tok_setup()
    _L0_tok_in = {k: v for k, v in _L0_tok_all.items() if k in ('weight', 'weighted_sum')}
    del _L0_tok_all

    def _L0_attn_setup():
        import jax, jax.numpy as jnp
        import numpy as np
        B, T, D = (4, 1024, 256)
        key = jax.random.key(seed)
        kx, kq, kk, kv = jax.random.split(key, 4)
        return {'x': jax.random.normal(kx, (B, T, D), dtype=jnp.float32), 'w_q': jax.random.normal(kq, (D, D), dtype=jnp.float32), 'w_k': jax.random.normal(kk, (D, D), dtype=jnp.float32), 'w_v': jax.random.normal(kv, (D, D), dtype=jnp.float32)}
    _L0_attn_all = _L0_attn_setup()
    _L0_attn_in = {k: v for k, v in _L0_attn_all.items() if k in ('w_q', 'w_k', 'w_v')}
    del _L0_attn_all

    def _L0_ffn_setup():
        import jax, jax.numpy as jnp
        import numpy as np
        DIM = 256

        def _reference_tuple_inner(x, W_r, W_k, W_v, mu_r, mu_k):
            B, T, C = x.shape
            x_prev = jnp.concatenate([jnp.zeros((B, 1, C), x.dtype), x[:, :-1, :]], axis=1)
            xr = mu_r * x + (1.0 - mu_r) * x_prev
            xk = mu_k * x + (1.0 - mu_k) * x_prev
            r = jax.nn.sigmoid(jnp.einsum('btc,dc->btd', xr, W_r))
            k = jnp.einsum('btc,dc->btd', xk, W_k)
            k_act = jnp.square(jax.nn.relu(k))
            out = r * jnp.einsum('btc,dc->btd', k_act, W_v)
            new_state = x[:, -1, :]
            return (out, new_state)
        key = jax.random.key(seed)
        ks = jax.random.split(key, 6)
        B, T, C = (8, 512, DIM)
        x = jax.random.normal(ks[0], (B, T, C), dtype=jnp.float32)
        s = 1.0 / np.sqrt(C)
        W_r = jax.random.uniform(ks[1], (C, C), jnp.float32, -s, s)
        W_k = jax.random.uniform(ks[2], (C, C), jnp.float32, -s, s)
        W_v = jax.random.uniform(ks[3], (C, C), jnp.float32, -s, s)
        mu_r = jax.random.uniform(ks[4], (C,), jnp.float32)
        mu_k = jax.random.uniform(ks[5], (C,), jnp.float32)
        return {'x': x, 'W_r': W_r, 'W_k': W_k, 'W_v': W_v, 'mu_r': mu_r, 'mu_k': mu_k}
    _L0_ffn_all = _L0_ffn_setup()
    _L0_ffn_in = {k: v for k, v in _L0_ffn_all.items() if k in ('W_r', 'W_k', 'W_v', 'mu_r', 'mu_k')}
    del _L0_ffn_all

    def _L1_attn_setup():
        import jax, jax.numpy as jnp
        import numpy as np
        B, T, C = (4, 1024, 256)
        key = jax.random.key(seed)
        ks = jax.random.split(key, 6)
        s = 1.0 / np.sqrt(C)
        x = jax.random.normal(ks[0], (B, T, C), dtype=jnp.float32)
        Wi = jax.random.uniform(ks[1], (C, C), jnp.float32, -s, s)
        bi = jax.random.uniform(ks[2], (C,), jnp.float32, -s, s)
        Wr = jax.random.uniform(ks[3], (C, C), jnp.float32, -s, s)
        br = jax.random.uniform(ks[4], (C,), jnp.float32, -s, s)
        cap_lambda = jax.random.uniform(ks[5], (1,), jnp.float32, 0.9, 0.999)
        return {'x': x, 'Wi': Wi, 'bi': bi, 'Wr': Wr, 'br': br, 'cap_lambda': cap_lambda}
    _L1_attn_all = _L1_attn_setup()
    _L1_attn_in = {k: v for k, v in _L1_attn_all.items() if k in ('Wi', 'bi', 'Wr', 'br', 'cap_lambda')}
    del _L1_attn_all

    def _L1_ffn_setup():
        import jax, jax.numpy as jnp
        import numpy as np
        from math import sqrt
        B, S, D, H, E, K, FF = (2, 256, 256, 16, 8, 2, 1024)
        HD = D // H
        EPS = 1e-05

        def _rope_cache(seq_len, hd):
            inv_freq = 1.0 / 10000.0 ** (jnp.arange(0, hd, 2, dtype=jnp.float32) / hd)
            t = jnp.arange(seq_len, dtype=jnp.float32)
            freqs = t[:, None] * inv_freq[None, :]
            emb = jnp.concatenate([freqs, freqs], axis=-1)
            return (jnp.cos(emb), jnp.sin(emb))

        def _rotate_half(x):
            x1, x2 = jnp.split(x, 2, axis=-1)
            return jnp.concatenate([-x2, x1], axis=-1)

        def _layernorm(x, g, b):
            m = jnp.mean(x, axis=-1, keepdims=True)
            v = jnp.var(x, axis=-1, keepdims=True)
            return (x - m) * jax.lax.rsqrt(v + EPS) * g + b

        def _forward(x, Wq, bq, Wk, bk, Wv, bv, Wo, bo, Wg, bg, W1, b1, W2, b2, g1, be1, g2, be2):
            bsz, seq, d = x.shape
            q = (x @ Wq + bq).reshape(bsz, seq, H, HD).transpose(0, 2, 1, 3)
            k = (x @ Wk + bk).reshape(bsz, seq, H, HD).transpose(0, 2, 1, 3)
            v = (x @ Wv + bv).reshape(bsz, seq, H, HD).transpose(0, 2, 1, 3)
            cos, sin = _rope_cache(seq, HD)
            cos = cos[None, None]
            sin = sin[None, None]
            q = q * cos + _rotate_half(q) * sin
            k = k * cos + _rotate_half(k) * sin
            scores = jnp.einsum('bhqd,bhkd->bhqk', q, k) / sqrt(HD)
            attn = jax.nn.softmax(scores, axis=-1)
            ao = jnp.einsum('bhqk,bhkd->bhqd', attn, v)
            ao = ao.transpose(0, 2, 1, 3).reshape(bsz, seq, d)
            attn_out = ao @ Wo + bo
            x1 = _layernorm(x + attn_out, g1, be1)
            gate_logits = x1 @ Wg + bg
            gate_probs = jax.nn.softmax(gate_logits, axis=-1)
            topk_p, topk_i = jax.lax.top_k(gate_probs, K)
            topk_p = topk_p / jnp.sum(topk_p, axis=-1, keepdims=True)
            comb = jnp.sum(jax.nn.one_hot(topk_i, E, dtype=x.dtype) * topk_p[..., None], axis=-2)
            h = jax.nn.gelu(jnp.einsum('bsd,edf->bsef', x1, W1) + b1, approximate=False)
            y = jnp.einsum('bsef,efd->bsed', h, W2) + b2
            moe_out = jnp.einsum('bse,bsed->bsd', comb, y)
            return _layernorm(x1 + moe_out, g2, be2)
        key = jax.random.key(seed)
        ks = jax.random.split(key, 20)
        std = 0.02
        p = lambda k, sh: jax.random.normal(k, sh, dtype=jnp.float32) * std
        return {'x': jax.random.normal(ks[0], (B, S, D), dtype=jnp.float32), 'Wq': p(ks[1], (D, D)), 'bq': jnp.zeros((D,), jnp.float32), 'Wk': p(ks[2], (D, D)), 'bk': jnp.zeros((D,), jnp.float32), 'Wv': p(ks[3], (D, D)), 'bv': jnp.zeros((D,), jnp.float32), 'Wo': p(ks[4], (D, D)), 'bo': jnp.zeros((D,), jnp.float32), 'Wg': p(ks[5], (D, E)), 'bg': jnp.zeros((E,), jnp.float32), 'W1': p(ks[6], (E, D, FF)), 'b1': jnp.zeros((E, FF), jnp.float32), 'W2': p(ks[7], (E, FF, D)), 'b2': jnp.zeros((E, D), jnp.float32), 'g1': jnp.ones((D,), jnp.float32), 'be1': jnp.zeros((D,), jnp.float32), 'g2': jnp.ones((D,), jnp.float32), 'be2': jnp.zeros((D,), jnp.float32)}
    _L1_ffn_all = _L1_ffn_setup()
    _L1_ffn_in = {k: v for k, v in _L1_ffn_all.items() if k in ('Wq', 'bq', 'Wk', 'bk', 'Wv', 'bv', 'Wo', 'bo', 'Wg', 'bg', 'W1', 'b1', 'W2', 'b2', 'g1', 'be1', 'g2', 'be2')}
    del _L1_ffn_all
    return {'x': x, 'L0_tok_weight': _L0_tok_in['weight'], 'L0_tok_weighted_sum': _L0_tok_in['weighted_sum'], 'L0_attn_w_q': _L0_attn_in['w_q'], 'L0_attn_w_k': _L0_attn_in['w_k'], 'L0_attn_w_v': _L0_attn_in['w_v'], 'L0_ffn_W_r': _L0_ffn_in['W_r'], 'L0_ffn_W_k': _L0_ffn_in['W_k'], 'L0_ffn_W_v': _L0_ffn_in['W_v'], 'L0_ffn_mu_r': _L0_ffn_in['mu_r'], 'L0_ffn_mu_k': _L0_ffn_in['mu_k'], 'L1_attn_Wi': _L1_attn_in['Wi'], 'L1_attn_bi': _L1_attn_in['bi'], 'L1_attn_Wr': _L1_attn_in['Wr'], 'L1_attn_br': _L1_attn_in['br'], 'L1_attn_cap_lambda': _L1_attn_in['cap_lambda'], 'L1_ffn_Wq': _L1_ffn_in['Wq'], 'L1_ffn_bq': _L1_ffn_in['bq'], 'L1_ffn_Wk': _L1_ffn_in['Wk'], 'L1_ffn_bk': _L1_ffn_in['bk'], 'L1_ffn_Wv': _L1_ffn_in['Wv'], 'L1_ffn_bv': _L1_ffn_in['bv'], 'L1_ffn_Wo': _L1_ffn_in['Wo'], 'L1_ffn_bo': _L1_ffn_in['bo'], 'L1_ffn_Wg': _L1_ffn_in['Wg'], 'L1_ffn_bg': _L1_ffn_in['bg'], 'L1_ffn_W1': _L1_ffn_in['W1'], 'L1_ffn_b1': _L1_ffn_in['b1'], 'L1_ffn_W2': _L1_ffn_in['W2'], 'L1_ffn_b2': _L1_ffn_in['b2'], 'L1_ffn_g1': _L1_ffn_in['g1'], 'L1_ffn_be1': _L1_ffn_in['be1'], 'L1_ffn_g2': _L1_ffn_in['g2'], 'L1_ffn_be2': _L1_ffn_in['be2']}

def reference(x, L0_tok_weight, L0_tok_weighted_sum, L0_attn_w_q, L0_attn_w_k, L0_attn_w_v, L0_ffn_W_r, L0_ffn_W_k, L0_ffn_W_v, L0_ffn_mu_r, L0_ffn_mu_k, L1_attn_Wi, L1_attn_bi, L1_attn_Wr, L1_attn_br, L1_attn_cap_lambda, L1_ffn_Wq, L1_ffn_bq, L1_ffn_Wk, L1_ffn_bk, L1_ffn_Wv, L1_ffn_bv, L1_ffn_Wo, L1_ffn_bo, L1_ffn_Wg, L1_ffn_bg, L1_ffn_W1, L1_ffn_b1, L1_ffn_W2, L1_ffn_b2, L1_ffn_g1, L1_ffn_be1, L1_ffn_g2, L1_ffn_be2):
    import jax
    import jax.numpy as jnp

    def _L0_tok_ref(x, weight, weighted_sum):
        import jax, jax.numpy as jnp
        import numpy as np
        return jnp.einsum('bhid,oi,od->bho', x, weighted_sum, weight)

    def _L0_attn_ref(x, w_q, w_k, w_v):
        import jax, jax.numpy as jnp
        import numpy as np
        B, T, D = (4, 1024, 256)
        q = jnp.einsum('btk,kd->btd', x, w_q)
        k = jnp.einsum('btk,kd->btd', x, w_k)
        v = jnp.einsum('btk,kd->btd', x, w_v)
        d = x.shape[-1]
        gamma = jnp.sqrt(jnp.asarray(d, dtype=x.dtype))
        a = jnp.einsum('bqd,bkd->bqk', q, k) * gamma
        y = jnp.einsum('bqt,btd->bqd', a, v)
        return y

    def _L0_ffn_ref(x, W_r, W_k, W_v, mu_r, mu_k):
        import jax, jax.numpy as jnp
        import numpy as np
        DIM = 256

        def _reference_tuple_inner(x, W_r, W_k, W_v, mu_r, mu_k):
            B, T, C = x.shape
            x_prev = jnp.concatenate([jnp.zeros((B, 1, C), x.dtype), x[:, :-1, :]], axis=1)
            xr = mu_r * x + (1.0 - mu_r) * x_prev
            xk = mu_k * x + (1.0 - mu_k) * x_prev
            r = jax.nn.sigmoid(jnp.einsum('btc,dc->btd', xr, W_r))
            k = jnp.einsum('btc,dc->btd', xk, W_k)
            k_act = jnp.square(jax.nn.relu(k))
            out = r * jnp.einsum('btc,dc->btd', k_act, W_v)
            new_state = x[:, -1, :]
            return (out, new_state)
        return _reference_tuple_inner(x, W_r, W_k, W_v, mu_r, mu_k)[0]

    def _L1_attn_ref(x, Wi, bi, Wr, br, cap_lambda):
        import jax, jax.numpy as jnp
        import numpy as np
        B, T, C = (4, 1024, 256)
        it = jax.nn.sigmoid(jnp.einsum('btc,dc->btd', x, Wi) + bi)
        rt = jax.nn.sigmoid(jnp.einsum('btc,dc->btd', x, Wr) + br)
        at = jnp.exp(-8.0 * jax.nn.softplus(cap_lambda) * rt)
        gx = jnp.sqrt(1.0 - at ** 2) * (it * x)

        def step(h, inp):
            a, g = inp
            h = a * h + g
            return (h, h)
        _, ys = jax.lax.scan(step, jnp.zeros((x.shape[0], x.shape[2]), x.dtype), (jnp.swapaxes(at, 0, 1), jnp.swapaxes(gx, 0, 1)))
        return jnp.swapaxes(ys, 0, 1)

    def _L1_ffn_ref(x, Wq, bq, Wk, bk, Wv, bv, Wo, bo, Wg, bg, W1, b1, W2, b2, g1, be1, g2, be2):
        import jax, jax.numpy as jnp
        import numpy as np
        from math import sqrt
        B, S, D, H, E, K, FF = (2, 256, 256, 16, 8, 2, 1024)
        HD = D // H
        EPS = 1e-05

        def _rope_cache(seq_len, hd):
            inv_freq = 1.0 / 10000.0 ** (jnp.arange(0, hd, 2, dtype=jnp.float32) / hd)
            t = jnp.arange(seq_len, dtype=jnp.float32)
            freqs = t[:, None] * inv_freq[None, :]
            emb = jnp.concatenate([freqs, freqs], axis=-1)
            return (jnp.cos(emb), jnp.sin(emb))

        def _rotate_half(x):
            x1, x2 = jnp.split(x, 2, axis=-1)
            return jnp.concatenate([-x2, x1], axis=-1)

        def _layernorm(x, g, b):
            m = jnp.mean(x, axis=-1, keepdims=True)
            v = jnp.var(x, axis=-1, keepdims=True)
            return (x - m) * jax.lax.rsqrt(v + EPS) * g + b

        def _forward(x, Wq, bq, Wk, bk, Wv, bv, Wo, bo, Wg, bg, W1, b1, W2, b2, g1, be1, g2, be2):
            bsz, seq, d = x.shape
            q = (x @ Wq + bq).reshape(bsz, seq, H, HD).transpose(0, 2, 1, 3)
            k = (x @ Wk + bk).reshape(bsz, seq, H, HD).transpose(0, 2, 1, 3)
            v = (x @ Wv + bv).reshape(bsz, seq, H, HD).transpose(0, 2, 1, 3)
            cos, sin = _rope_cache(seq, HD)
            cos = cos[None, None]
            sin = sin[None, None]
            q = q * cos + _rotate_half(q) * sin
            k = k * cos + _rotate_half(k) * sin
            scores = jnp.einsum('bhqd,bhkd->bhqk', q, k) / sqrt(HD)
            attn = jax.nn.softmax(scores, axis=-1)
            ao = jnp.einsum('bhqk,bhkd->bhqd', attn, v)
            ao = ao.transpose(0, 2, 1, 3).reshape(bsz, seq, d)
            attn_out = ao @ Wo + bo
            x1 = _layernorm(x + attn_out, g1, be1)
            gate_logits = x1 @ Wg + bg
            gate_probs = jax.nn.softmax(gate_logits, axis=-1)
            topk_p, topk_i = jax.lax.top_k(gate_probs, K)
            topk_p = topk_p / jnp.sum(topk_p, axis=-1, keepdims=True)
            comb = jnp.sum(jax.nn.one_hot(topk_i, E, dtype=x.dtype) * topk_p[..., None], axis=-2)
            h = jax.nn.gelu(jnp.einsum('bsd,edf->bsef', x1, W1) + b1, approximate=False)
            y = jnp.einsum('bsef,efd->bsed', h, W2) + b2
            moe_out = jnp.einsum('bse,bsed->bsd', comb, y)
            return _layernorm(x1 + moe_out, g2, be2)
        return _forward(x, Wq, bq, Wk, bk, Wv, bv, Wo, bo, Wg, bg, W1, b1, W2, b2, g1, be1, g2, be2)
    h = _L0_tok_ref(x, L0_tok_weight, L0_tok_weighted_sum)
    h = _layernorm(h + _L0_attn_ref(h, L0_attn_w_q, L0_attn_w_k, L0_attn_w_v), axis=-1)
    h = _layernorm(h + _L0_ffn_ref(h, L0_ffn_W_r, L0_ffn_W_k, L0_ffn_W_v, L0_ffn_mu_r, L0_ffn_mu_k), axis=-1)
    h = _layernorm(h + _L1_attn_ref(h, L1_attn_Wi, L1_attn_bi, L1_attn_Wr, L1_attn_br, L1_attn_cap_lambda), axis=-1)
    h = _layernorm(h + _L1_ffn_ref(h, L1_ffn_Wq, L1_ffn_bq, L1_ffn_Wk, L1_ffn_bk, L1_ffn_Wv, L1_ffn_bv, L1_ffn_Wo, L1_ffn_bo, L1_ffn_Wg, L1_ffn_bg, L1_ffn_W1, L1_ffn_b1, L1_ffn_W2, L1_ffn_b2, L1_ffn_g1, L1_ffn_be1, L1_ffn_g2, L1_ffn_be2), axis=-1)
    return h

_drawn_inputs = setup_inputs


def setup_inputs(seed=0):
    import zlib

    import numpy as np

    out = dict(_drawn_inputs(seed))
    spreads = {'L1_ffn_bq': (0.0, 0.8),
     'L1_ffn_bk': (0.0, 0.8),
     'L1_ffn_bv': (0.0, 0.464),
     'L1_ffn_bo': (0.0, 0.1),
     'L1_ffn_bg': (0.0, 0.1),
     'L1_ffn_b1': (0.0, 0.617),
     'L1_ffn_b2': (0.0, 0.1),
     'L1_ffn_g1': (1.0, 0.2),
     'L1_ffn_be1': (0.0, 0.1),
     'L1_ffn_g2': (1.0, 0.2),
     'L1_ffn_be2': (0.0, 0.1)}
    factors = {'L0_ffn_W_r': 3.006,
     'L0_ffn_mu_r': 5.793,
     'L1_attn_bi': 8.0,
     'L1_attn_Wr': 3.527,
     'L1_attn_br': 8.0,
     'L1_ffn_Wq': 8.0,
     'L1_ffn_Wk': 8.0,
     'L1_ffn_Wv': 8.0,
     'L1_ffn_Wo': 3.206}
    for name, (base, spread) in spreads.items():
        noise = np.random.default_rng([zlib.crc32(name.encode()), seed]).standard_normal(out[name].shape)
        drawn = base * np.exp(spread * noise) if base else spread * noise
        out[name] = jnp.asarray(drawn.astype(out[name].dtype))
    for name, factor in factors.items():
        out[name] = (out[name] * factor).astype(out[name].dtype)
    return out
```

```python
from contextlib import ExitStack

import concourse.bass as bass
from concourse import mybir

F32 = mybir.dt.float32
F32R = mybir.dt.float32r
I32 = mybir.dt.int32
U32 = mybir.dt.uint32
ALU = mybir.AluOpType
ACT = mybir.ActivationFunctionType
AX_X = mybir.AxisListType.X

P = 128
B, T, D = 8, 512, 256
DP = 4
LANES = 2
ITERS = B // LANES
TT = T // P
KC = D // P
H, HD = 16, 16
E, FF = 8, 1024
FC = FF // P
TILES = B * TT
GROUPS = H // 4
EPS = 1e-5
NORMS = 4
N_LOADS = 28
DVE_LINKS = 114
ACT_LINKS = 2
STACK_DMAS = 14
LINKS3 = 18
REGION = B * T + P
ROWS = E * REGION + E * P
STEPS = B * T * 2 // P + E
SLOTS = 3
AV = (3, 4)
PARTS = 3
ROW_MAX = PARTS * HD
SETUP_MATS = 3
MATS = ("ws", "wq", "wk", "fr", "fk", "fv", "ai", "ar")


def psum_plan():
    def place(keys):
        at, used, out = 0, [0] * 5, {}
        for key, slot in keys:
            if slot is None:
                slot = at % SLOTS
                at += 1
            out[key] = (slot, used[slot])
            used[slot] += 1
        return out, used

    setup = [(("wT", m), None) for m in MATS] + [(("at",), None)]
    turn = []
    for lane in range(LANES):
        turn.append((("tok", lane), 2))
        turn += [(("xT", lane, tt), tt % 2) for tt in range(TT)]
    for stage in ("hT0", "g", "gv", "b", "y", "hT1", "r", "k", "kv", "hT2", "it", "rt", "back", "hT3",
                  "qk0", "qk1", "v"):
        turn += [((stage, lane), None) for lane in range(LANES)]
    turn += [((f"qkT{half}", lane), None) for lane in range(LANES) for half in range(2)]
    turn += [(key, slot) for key, slot in attention_order() if slot != "av"]
    for stage in ("aoT", "wo", "xT1", "gate", "rank"):
        turn += [((stage, lane), None) for lane in range(LANES)]
    av = [(("av", lane, g), AV[g % 2]) for lane in range(LANES) for g in range(GROUPS)]
    s, s_used = place(setup)
    t, t_used = place(turn + av)
    return s, s_used, t, t_used


def attention_order():
    groups = [(lane, g) for lane in range(LANES) for g in range(GROUPS)]
    out = []
    for step in range(len(groups) + 2):
        ahead = groups[step] if step < len(groups) else None
        now = groups[step - 2] if step >= 2 else None
        for n in range(8):
            if ahead:
                out.append((("max",) + ahead + (n,), None))
            if now:
                out.append((("exp",) + now + (n,), None))
            if n == 3 and step >= 3:
                out.append((("avT",) + groups[step - 3], None))
        if ahead:
            out.append((("maxT",) + ahead, None))
        if now:
            out.append((("av",) + now, "av"))
        if step == len(groups) + 1:
            out.append((("avT",) + now, None))
    return out


class Count:

    def __init__(self, sem, base=0):
        self.sem, self.base, self.n = sem, base, 0

    def link(self, eng, ins):
        self.n += 1
        ins.then_inc(self.sem, 1)
        eng.wait_ge(self.sem, self.base + self.n)


def tower(nc, a, out):
    with ExitStack() as ctx:
        def sem(name):
            return ctx.enter_context(nc.semaphore(name))

        def sems(name, n=LANES):
            return [sem(f"{name}{j}") for j in range(n)]

        plan_setup, used_setup, plan, used = psum_plan()
        ps = ctx.enter_context(nc.psum_tensor("ps", [P, 8, 512], F32))

        def granule(slot):
            return ps[:, 2 * slot:2 * slot + 2, :] if slot < SLOTS else ps[:, slot + SLOTS, :]

        filled, drained = sems("psum_filled", 5), sems("psum_drained", 5)

        def slot_of(key, i):
            return (plan_setup if i is None else plan)[key][0]

        def fill_value(key, i):
            if i is None:
                return plan_setup[key][1] + 1
            slot, n = plan[key]
            return used_setup[slot] + n + 1 + i * used[slot]

        def room(eng, key, i):
            slot = slot_of(key, i)
            eng.wait_ge(drained[slot], fill_value(key, i))
            return granule(slot)

        def full(eng, key, i):
            slot = slot_of(key, i)
            eng.wait_ge(filled[slot], fill_value(key, i))
            return granule(slot)

        def copied(eng, key, i):
            slot = slot_of(key, i)
            eng.wait_ge(drained[slot], fill_value(key, i) + 1)

        def fill_sem(key, i):
            return filled[slot_of(key, i)]

        def drain_sem(key, i):
            return drained[slot_of(key, i)]

        def sbuf(stack, name, shape, dt=F32):
            return stack.enter_context(nc.sbuf_tensor(name, shape, dt))

        def dram(name, shape, dt=F32):
            return nc.dram_tensor(name, shape, dt, kind="Internal").ap()

        qk_parts = dram("qk_parts", (LANES, 2, 2 * D, T))
        mx_parts = dram("mx_parts", (LANES, GROUPS, 2, 4, T))
        xs = dram("xs", (ROWS, D))
        ys = dram("ys", (STEPS * P, D))
        h3_all = dram("h3_all", (B * T, D))
        x1_all = dram("x1_all", (B * T, D))

        ident = sbuf(ctx, "ident", [P, P])
        slots_all = sbuf(ctx, "slots_all", [P, TILES, 2], I32)
        topw_all = sbuf(ctx, "topw_all", [P, TILES, 2])
        run = sbuf(ctx, "run", [P, E])

        p1 = ctx.enter_context(ExitStack())
        NL = range(LANES)
        wT = sbuf(p1, "wT", [P, len(MATS) - SETUP_MATS, KC, D])
        wc = sbuf(p1, "wc", [P, DP * 2, D])
        wv0 = sbuf(p1, "wv0", [P, KC, D])
        at16 = sbuf(p1, "at16", [P, KC, D])
        wqk = sbuf(p1, "wqk", [P, KC, 2 * D])
        wv1 = sbuf(p1, "wv1", [P, KC, D])
        wo = sbuf(p1, "wo", [P, KC, D])
        bo = sbuf(p1, "bo", [P, D])
        wg = sbuf(p1, "wg", [P, KC, E])
        bqk = sbuf(p1, "bqk", [P, 2 * D])
        bv = sbuf(p1, "bv", [P, D])
        bg = sbuf(p1, "bg", [P, E])
        g1t = sbuf(p1, "g1t", [P, D])
        be1t = sbuf(p1, "be1t", [P, D])
        rope = sbuf(p1, "rope", [P, 2, TT, HD])
        cols = sbuf(p1, "cols", [P, 4, KC])
        ncols = sbuf(p1, "ncols", [P, 4, KC])
        cap = sbuf(p1, "cap", [P, 8])
        ntri = sbuf(p1, "ntri", [P, P])
        ones = sbuf(p1, "ones", [P, P])
        region = sbuf(p1, "region", [P, E])
        iota8 = sbuf(p1, "iota8", [P, E])
        half = sbuf(p1, "half", [P, TT])
        xin = sbuf(p1, "xin", [P, TT, D * DP])
        wnat = xin[:].rearrange("p t n -> p (t n)").rearrange("p (m c n) -> p m c n", m=len(MATS), c=KC)
        pt = sbuf(p1, "pt", [P, 2, 2 * T])
        xT = [pt[:, j].rearrange("p (k t) -> p k t", k=2 * DP) for j in range(2)]
        wb = pt[:, 0].rearrange("p (o d) -> p o d", d=DP)
        h = [sbuf(p1, f"h{l}", [P, TT, D]) for l in NL]
        hT = [sbuf(p1, f"hT{l}", [P, KC, T + 1]) for l in NL]
        s = [sbuf(p1, f"s{l}", [P, TT, D]) for l in NL]
        w12 = [sbuf(p1, f"w12_{l}", [P, 4, T]) for l in NL]
        wT0 = w12[0][:].rearrange("p a n -> p (a n)")[:, 0:SETUP_MATS * KC * D].rearrange(
            "p (m c n) -> p m c n", m=SETUP_MATS, c=KC)
        probs = [pt[:, j].rearrange("p (a n) -> p a n", a=2) for j in range(2)] + [hT[l][:, :, 1:T + 1] for l in NL]
        w3 = [sbuf(p1, f"w3_{l}", [P, KC, T]) for l in NL]
        stats = [sbuf(p1, f"stats{l}", [P, TT, 6]) for l in NL]
        mv = [sbuf(p1, f"mv{l}", [P, TT, 2]) for l in NL]
        ve = [sbuf(p1, f"ve{l}", [P, TT]) for l in NL]
        rstd = [sbuf(p1, f"rstd{l}", [P, TT]) for l in NL]
        qkhi = pt[:].rearrange("p a (b n) -> p (a b) n", b=2).bitcast(F32R)
        qklo = sbuf(p1, "qklo", [P, 4, T], F32R)
        qst = sbuf(p1, "qst", [P, GROUPS, 2, T], F32R)
        kst = sbuf(p1, "kst", [P, GROUPS, 4, T], F32R)
        vp = [sbuf(p1, f"vp{l}", [P, TT, H, 2 * HD]) for l in NL]
        mx = sbuf(p1, "mx", [P, 2, TT, 4])
        mhl = qklo[0:4, 0:2, :]
        gl = [sbuf(p1, f"gl{l}", [P, 6, TT, E]) for l in NL]
        gm = [sbuf(p1, f"gm{l}", [P, 4, TT]) for l in NL]
        top8 = [sbuf(p1, f"top8{l}", [P, TT, 8]) for l in NL]
        idx8 = [sbuf(p1, f"idx8{l}", [P, TT, 8], U32) for l in NL]
        idxf = [sbuf(p1, f"idxf{l}", [P, TT, 2]) for l in NL]
        slot_i = [sbuf(p1, f"slot_i{l}", [P, TT, 2], I32) for l in NL]

        def by_token(ap):
            return ap.rearrange("p a n -> p (a n)").rearrange("p (t d) -> p t d", t=TT)

        def flat(ap):
            return ap.rearrange("p a n -> p (a n)")

        xr, xk = [w12[l][:, 0:2] for l in NL], [w12[l][:, 2:4] for l in NL]
        num = [s[l][:].rearrange("p t d -> p (t d)").rearrange("p (g q) -> p g q", g=2) for l in NL]
        ao = [w12[l][:, 0:2].rearrange("p a n -> p (a n)").rearrange("p (t d) -> p t d", t=TT) for l in NL]
        aoT = [w12[l][:, 2:4] for l in NL]
        rden = [sbuf(p1, f"rden{l}", [P, TT, 4]) for l in NL]
        G = [w12[l][:, 0:2, 0:D] for l in NL]
        GV = [w3[l][:, :, 0:D] for l in NL]
        BM = [w12[l][:, 2:4, 0:D] for l in NL]

        w_loaded = sem("weights_loaded")
        pool_setup, dve_setup, act_setup = sem("pool_setup"), sem("dve_setup"), sem("act_setup")
        dve_own, act_own = sem("dve_own"), sem("act_own")
        x_loaded, x_used = sems("x_loaded", TT), sems("x_used", TT)
        h_ready = [sems(f"h_ready{l}_", 5) for l in NL]
        var_ready, rstd_ready = sems("var_ready"), sems("rstd_ready")
        mix_ready = sems("mix_ready")
        relu_sq, at_ready = sems("relu_squared"), sems("at_ready")
        a2_ready, a2_capped, sq_ready = sems("a2_ready"), sems("a2_capped"), sems("sqrt_ready")
        sT_ready = sems("scan_ready")
        h3_stored, x1_stored = sems("h3_stored"), sems("x1_stored")
        qkb_ready, swapped, qk_ready = sems("qk_biased"), sems("qk_swapped"), sems("qk_turned")
        hi_ready, lo_ready = sem("hi_ready"), sem("lo_ready")
        parts_stored, v_ready = sems("parts_stored"), sems("v_ready")
        st_loaded, st_used = sems("stack_loaded", GROUPS), sems("stack_used", GROUPS)
        av_copied, bo_added = sems("av_copied"), sems("bo_added")
        mhl_ready, mx_stored, mx_loaded = sem("mx_parts"), sem("mx_stored"), sems("mx_loaded", GROUPS)
        ao_ready = sems("ao_ready")
        gate_in, gate_exp, mask_ready = sems("gate_in"), sems("gate_exp"), sems("mask_ready")
        slot_ready, scattered, rows_away = sems("slot_ready"), sems("scattered"), sems("rows_away")
        settled, settled_pool = sem("settled"), sem("settled_pool")

        block = p1.enter_context(nc.Block())

        def mat(n):
            return MATS.index(n)

        def rows(ap):
            return ap.rearrange("(c p) n -> p c n", p=P)

        def bcast(ap, n):
            return ap.rearrange("(o n) -> o n", o=1).broadcast_to([P, n])

        LOADS = []
        for n, name in zip(MATS, ("L0_tok_weighted_sum", "L0_attn_w_q", "L0_attn_w_k", "L0_ffn_W_r",
                                  "L0_ffn_W_k", "L0_ffn_W_v", "L1_attn_Wi", "L1_attn_Wr")):
            LOADS.append((wnat[:, mat(n)], rows(a[name])))
        LOADS += [(wv0[:], rows(a["L0_attn_w_v"])), (wqk[:, :, 0:D], rows(a["L1_ffn_Wq"])),
                  (wqk[:, :, D:2 * D], rows(a["L1_ffn_Wk"])), (wv1[:], rows(a["L1_ffn_Wv"])),
                  (wg[:], rows(a["L1_ffn_Wg"])), (wo[:], rows(a["L1_ffn_Wo"])), (bo[:], bcast(a["L1_ffn_bo"], D)),
                  (wb[:].rearrange("p o d -> p (o d)"), bcast(a["L0_tok_weight"].rearrange("o d -> (o d)"), D * DP)),
                  (bqk[:, 0:D], bcast(a["L1_ffn_bq"], D)), (bqk[:, D:2 * D], bcast(a["L1_ffn_bk"], D)),
                  (bv[:], bcast(a["L1_ffn_bv"], D)), (bg[:], bcast(a["L1_ffn_bg"], E)),
                  (g1t[:], bcast(a["L1_ffn_g1"], D)), (be1t[:], bcast(a["L1_ffn_be1"], D)),
                  (cap[:, 0:1], bcast(a["L1_attn_cap_lambda"], 1)),
                  (rope[:], a["rope"].rearrange("c (t p) d -> p c t d", p=P))]
        for j, name in enumerate(("L0_ffn_mu_r", "L0_ffn_mu_k", "L1_attn_bi", "L1_attn_br")):
            LOADS.append((cols[:, j, :], a[name].rearrange("(c p) -> p c", p=P)))

        x_src = a["x"].rearrange("b (t p) i d -> b t p (i d)", p=P)

        @block.sync
        def _(sp):
            with nc.allow_non_contiguous_dma(reason="columns and broadcasts of small weights, once"):
                for dst, src in LOADS:
                    sp.dma_start(dst, src).then_inc(w_loaded, 16)
            full(sp, ("at",), None)
            with sp.Fori(0, ITERS) as i:
                for l in NL:
                    for tt in range(TT):
                        sp.wait_ge(x_used[tt], i * LANES + l + 1)
                        sp.dma_start(xin[:, tt, :], x_src[bass.ds(i * LANES + l, 1), tt].rearrange("o p n -> (o p) n")
                                     ).then_inc(x_loaded[tt], 16)
                for l in NL:
                    sp.wait_ge(h_ready[l][3], i + 1)
                    sp.dma_start(h3_all.rearrange("(b t p) d -> b p t d", t=TT, p=P)[bass.ds(i * LANES + l, 1)].rearrange("o p t d -> (o p) t d"),
                                 h[l][:]).then_inc(h3_stored[l], 16)
                for l in NL:
                    sp.wait_ge(hi_ready, 4 * i + 2 * l + 2)
                    sp.dma_start(qk_parts[l, 0].rearrange("(c p) t -> p c t", p=P), qkhi.bitcast(F32)).then_inc(parts_stored[l], 16)
                    sp.wait_ge(lo_ready, 4 * i + 2 * l + 2)
                    sp.dma_start(qk_parts[l, 1].rearrange("(c p) t -> p c t", p=P), qklo[:].bitcast(F32)).then_inc(parts_stored[l], 16)

                def load_stacks(l, g):
                    sp.wait_ge(parts_stored[l], 32 * i + 32)
                    sp.wait_ge(st_used[g], i * LANES + l + 1)
                    for e in range(2):
                        for part in range(PARTS):
                            p0 = 64 * e + HD * part
                            for base, kinds in ((0, (0, 1, 0)), (1, (0, 0, 1))):
                                src = qk_parts[l, kinds[part]].rearrange("(q g j e d) t -> q g e d j t", q=2, g=GROUPS, e=2, d=HD)[base, g, e]
                                dst = qst[p0:p0 + HD, g] if base == 0 else kst[p0:p0 + HD, g, e:4:2, :]
                                sp.dma_start(dst.bitcast(F32), src).then_inc(st_loaded[g], 16)
                        p0 = 64 * e + ROW_MAX
                        sp.dma_start(qst[p0:p0 + 2, g].bitcast(F32), kst[64:66, g, 0:4:2, :].bitcast(F32)).then_inc(st_loaded[g], 16)

                groups = [(l, g) for l in NL for g in range(GROUPS)]
                for l, g in groups[:GROUPS]:
                    load_stacks(l, g)
                for at, (l, g) in enumerate(groups):
                    n = i * LANES * GROUPS + at
                    sp.wait_ge(mhl_ready, n + 1)
                    sp.dma_start(mx_parts[l, g].rearrange("k h t -> h k t"), mhl.bitcast(F32)).then_inc(mx_stored, 16)
                    sp.wait_ge(mx_stored, n * 16 + 32)
                    for e in range(2):
                        src = mx_parts[l, g].rearrange("k (j e) t -> e k j t", e=2)[e]
                        p0 = 64 * e + ROW_MAX
                        sp.dma_start(qst[p0:p0 + 2, g].bitcast(F32), src).then_inc(mx_loaded[g], 16)
                    if 2 <= at < GROUPS + 2:
                        load_stacks(*groups[at + 2])
                for l in NL:
                    sp.wait_ge(h_ready[l][4], i + 1)
                    sp.dma_start(x1_all.rearrange("(b t p) d -> b p t d", t=TT, p=P)[bass.ds(i * LANES + l, 1)].rearrange("o p t d -> (o p) t d"),
                                 h[l][:]).then_inc(x1_stored[l], 16)
            for l in NL:
                sp.wait_ge(h3_stored[l], 16 * ITERS)
                sp.wait_ge(x1_stored[l], 16 * (ITERS + 1))
        @block.tensor
        def _(pe):
            mm, tr = nc.tensor.matmul, nc.tensor.transpose
            pe.wait_ge(pool_setup, 2)
            pe.wait_ge(w_loaded, 16 * N_LOADS)
            for m in MATS:
                g = room(pe, ("wT", m), None)
                for kc in range(KC):
                    for c in range(KC):
                        ins = tr(g[:, kc, c * P:(c + 1) * P], wnat[:, mat(m), c, kc * P:(kc + 1) * P], ident[:])
                ins.then_inc(fill_sem(("wT", m), None), 1)
            for m in ("wq", "wk"):
                copied(pe, ("wT", m), None)
            g = room(pe, ("at",), None)
            for kc in range(KC):
                for dc in range(KC):
                    ins = mm(g[:, 0, kc * D:(kc + 1) * D], wT0[:, mat("wk"), dc, kc * P:(kc + 1) * P],
                             wT0[:, mat("wq"), dc, :], start=dc == 0, stop=dc == KC - 1)
            ins.then_inc(fill_sem(("at",), None), 1)
            pe.wait_ge(dve_setup, 3)

            with pe.Fori(0, ITERS) as i:
                def to_channels(stage, l, src):
                    g = room(pe, (stage, l), i)
                    for dc in range(KC):
                        for tt in range(TT):
                            ins = tr(g[:, dc, tt * P:(tt + 1) * P], src[:, tt, dc * P:(dc + 1) * P], ident[:])
                    ins.then_inc(fill_sem((stage, l), i), 1)

                def by_tokens(stage, l, lhs, rhs, n=D):
                    g = flat(room(pe, (stage, l), i))
                    chunks = rhs.shape[1]
                    for tt in range(TT):
                        for kc in range(chunks):
                            ins = mm(g[:, tt * n:(tt + 1) * n], lhs[:, kc, tt * P:(tt + 1) * P], rhs[:, kc, :],
                                     start=kc == 0, stop=kc == chunks - 1)
                    ins.then_inc(fill_sem((stage, l), i), 1)

                def by_channels(stage, l, wt, rhs):
                    g = room(pe, (stage, l), i)
                    for dc in range(KC):
                        for kc in range(KC):
                            ins = mm(g[:, dc, :], wt[:, kc, dc * P:(dc + 1) * P], rhs[:, kc, :],
                                     start=kc == 0, stop=kc == KC - 1)
                    ins.then_inc(fill_sem((stage, l), i), 1)

                def square(stage, l, lhs, rhs, chunks):
                    g = room(pe, (stage, l), i)
                    for dc in range(KC):
                        for kc in range(chunks):
                            ins = mm(g[:, 0, dc * D:(dc + 1) * D], lhs[:, kc, dc * P:(dc + 1) * P], rhs[:, kc, :],
                                     start=kc == 0, stop=kc == chunks - 1)
                    ins.then_inc(fill_sem((stage, l), i), 1)

                for l in NL:
                    for tt in range(TT + 1):
                        if tt < TT:
                            pe.wait_ge(x_loaded[tt], 16 * (i * LANES + l + 1))
                            g = flat(room(pe, ("xT", l, tt), i)).rearrange("p (k t) -> p k t", t=P)
                            xv = xin[:, tt].rearrange("p (c q d) -> p d c q", c=2, d=DP)
                            for k in range(2 * DP):
                                ins = tr(g[:, k, :], xv[:, k // 2, k % 2, :], ident[:])
                            ins.then_inc(fill_sem(("xT", l, tt), i), 1)
                        if tt >= 1:
                            if tt == 1:
                                tok = flat(room(pe, ("tok", l), i))
                            t0 = tt - 1
                            copied(pe, ("xT", l, t0), i)
                            for k in range(2 * DP):
                                ins = mm(tok[:, t0 * D:(t0 + 1) * D], xT[t0 % 2][:, k, :], wc[:, k, :],
                                         start=k == 0, stop=k == 2 * DP - 1)
                                if k == 0:
                                    ins.then_inc(x_used[t0], 1)
                    ins.then_inc(fill_sem(("tok", l), i), 1)

                for l in NL:
                    pe.wait_ge(h_ready[l][0], i + 1)
                    to_channels("hT0", l, h[l])
                for l in NL:
                    square("g", l, h[l], h[l], TT)
                for l in NL:
                    copied(pe, ("g", l), i)
                    square("gv", l, G[l], wv0, KC)
                for l in NL:
                    copied(pe, ("gv", l), i)
                    square("b", l, at16, GV[l], KC)
                for l in NL:
                    copied(pe, ("b", l), i)
                    by_tokens("y", l, hT[l][:, :, 1:T + 1], BM[l])

                for l in NL:
                    pe.wait_ge(h_ready[l][1], i + 1)
                    to_channels("hT1", l, h[l])
                for l in NL:
                    pe.wait_ge(mix_ready[l], 2 * i + 1)
                    by_tokens("r", l, xr[l], wT[:, mat("fr") - SETUP_MATS])
                for l in NL:
                    pe.wait_ge(mix_ready[l], 2 * i + 2)
                    by_channels("k", l, wT[:, mat("fk") - SETUP_MATS], xk[l])
                for l in NL:
                    pe.wait_ge(relu_sq[l], i + 1)
                    by_tokens("kv", l, s[l][:].rearrange("p t d -> p (t d)").rearrange("p (c n) -> p c n", c=KC), wT[:, mat("fv") - SETUP_MATS])

                for l in NL:
                    pe.wait_ge(h_ready[l][2], i + 1)
                    to_channels("hT2", l, h[l])
                for l in NL:
                    copied(pe, ("hT2", l), i)
                    by_channels("it", l, wT[:, mat("ai") - SETUP_MATS], hT[l][:, :, 1:T + 1])
                for l in NL:
                    by_channels("rt", l, wT[:, mat("ar") - SETUP_MATS], hT[l][:, :, 1:T + 1])
                for l in NL:
                    pe.wait_ge(sT_ready[l], i + 1)
                    g = flat(room(pe, ("back", l), i))
                    for tt in range(TT):
                        for dc in range(KC):
                            ins = tr(g[:, tt * D + dc * P:tt * D + (dc + 1) * P], w3[l][:, dc, tt * P:(tt + 1) * P], ident[:])
                    ins.then_inc(fill_sem(("back", l), i), 1)

                for l in NL:
                    pe.wait_ge(h_ready[l][3], i + 1)
                    to_channels("hT3", l, h[l])
                for half_ in range(2):
                    for l in NL:
                        copied(pe, ("hT3", l), i)
                        g = room(pe, (f"qk{half_}", l), i)
                        for tb in range(2):
                            tt = 2 * half_ + tb
                            for kc in range(KC):
                                ins = mm(g[:, tb, :], hT[l][:, kc, 1 + tt * P:1 + (tt + 1) * P], wqk[:, kc, :],
                                         start=kc == 0, stop=kc == KC - 1)
                        ins.then_inc(fill_sem((f"qk{half_}", l), i), 1)
                for l in NL:
                    by_tokens("v", l, hT[l][:, :, 1:T + 1], wv1)
                for l in NL:
                    for half_ in range(2):
                        pe.wait_ge(qk_ready[l], i + 1)
                        g = room(pe, (f"qkT{half_}", l), i)
                        for c in range(2):
                            for tt in range(TT):
                                c0 = (2 * half_ + c) * P
                                ins = tr(g[:, c, tt * P:(tt + 1) * P], w12[l][:, tt, c0:c0 + P], ident[:])
                        ins.then_inc(fill_sem((f"qkT{half_}", l), i), 1)

                def values(l, g, kt):
                    copied(pe, ("exp", l, g, 2 * kt + 1), i)
                    av = ps[:, slot_of(("av", l, g), i) + SLOTS, :]
                    if kt == 0:
                        room(pe, ("av", l, g), i)
                        pe.wait_ge(v_ready[l], i + 1)
                    for j in range(4):
                        ins = mm(av[32 * j:32 * j + 32, :], vp[l][:, kt, 4 * g + j, :], probs[(2 * kt + j // 2) % 4][:, j % 2, :],
                                 start=kt == 0, stop=kt == TT - 1)
                    if kt == TT - 1:
                        ins.then_inc(fill_sem(("av", l, g), i), 1)

                late = []
                for key, _ in attention_order():
                    kind, l, g = key[:3]
                    if kind == "max":
                        if key[3] == 0:
                            pe.wait_ge(st_loaded[g], 16 * STACK_DMAS * (i * LANES + l + 1))
                        j, qh = key[3] // 2, key[3] % 2
                        out_ = room(pe, key, i)
                        for b_ in range(2):
                            qt = 2 * qh + b_
                            ins = mm(out_[:, b_, :], qst[:, g, j // 2, qt * P:(qt + 1) * P], kst[:, g, j, :], start=True, stop=True)
                        ins.then_inc(fill_sem(key, i), 1)
                    elif kind == "exp":
                        n = key[3]
                        if n == 0:
                            pe.wait_ge(mx_loaded[g], (i * LANES + l + 1) * 32)
                        kt, pair = n // 2, n % 2
                        out_ = room(pe, key, i)
                        for e in range(2):
                            ins = mm(out_[:, e, :], kst[:, g, 2 * pair + e, kt * P:(kt + 1) * P], qst[:, g, pair, :],
                                     start=True, stop=True)
                        ins.then_inc(fill_sem(key, i), 1)
                        if n == 7:
                            copied(pe, key, i)
                            pe.sem_inc(st_used[g], 1)
                        if n % 2 == 1:
                            late.append((l, g, kt))
                            if len(late) > 1:
                                values(*late.pop(0))
                    elif kind == "maxT":
                        copied(pe, ("max", l, g, 7), i)
                        out_ = room(pe, key, i)
                        for tt in range(TT):
                            ins = tr(out_[0:4, 0, tt * P:(tt + 1) * P], mx[:, g % 2, tt, :], ident[:])
                        ins.then_inc(fill_sem(key, i), 1)
                    elif kind == "avT":
                        pe.wait_ge(av_copied[l], GROUPS * i + g + 1)
                        out_ = room(pe, key, i)
                        for tt in range(TT):
                            ins = tr(out_[:, 0, tt * P:(tt + 1) * P], num[l][:, g % 2, tt * P:(tt + 1) * P], ident[:])
                        ins.then_inc(fill_sem(key, i), 1)
                    else:
                        while late:
                            values(*late.pop(0))

                for l in NL:
                    pe.wait_ge(ao_ready[l], GROUPS * (i + 1))
                    to_channels("aoT", l, ao[l])
                for l in NL:
                    copied(pe, ("aoT", l), i)
                    by_tokens("wo", l, aoT[l], wo)
                for l in NL:
                    pe.wait_ge(h_ready[l][4], i + 1)
                    to_channels("xT1", l, h[l])
                for l in NL:
                    copied(pe, ("xT1", l), i)
                    by_tokens("gate", l, hT[l][:, :, 1:T + 1], wg, n=E)
                for l in NL:
                    pe.wait_ge(mask_ready[l], i + 1)
                    g = flat(room(pe, ("rank", l), i))
                    mask = gl[l][:, 2].rearrange("p t e -> p (t e)")
                    mm(g[:, 0:TT * E], ntri[:], mask, start=True, stop=True)
                    mm(g[:, TT * E:2 * TT * E], ones[:], mask, start=True, stop=True
                       ).then_inc(fill_sem(("rank", l), i), 1)

        @block.scalar
        def _(act):
            fn = nc.scalar.activation
            act.wait_ge(dve_setup, 2)
            fn(cap[:, 2:3], cap[:, 1:2], ACT.Exp, scale=-1.0).then_inc(act_setup, 1)
            act.wait_ge(act_setup, 1)
            fn(cap[:, 3:4], cap[:, 2:3], ACT.Ln, bias=1.0).then_inc(act_setup, 1)
            act.wait_ge(dve_setup, 3)

            with act.Fori(0, ITERS) as i:
                own = Count(act_own, i * ACT_LINKS)

                def copy_out(key, dst):
                    src = full(act, key, i)
                    fn(dst, src, ACT.Copy).then_inc(drain_sem(key, i), 1)

                for l in NL:
                    for tt in range(0, TT, 2):
                        copy_out(("xT", l, tt), pt[:, tt % 2].rearrange("p (a n) -> p a n", a=2))
                    act.wait_ge(x1_stored[l], 16 * i + 16)
                    act.wait_ge(rows_away[l], i + 1)
                    src = by_token(full(act, ("tok", l), i))
                    own.link(act, fn(h[l][:], src, ACT.Copy))
                    act.sem_inc(h_ready[l][0], 1)
                    act.sem_inc(drain_sem(("tok", l), i), 1)
                for l in NL:
                    copy_out(("hT0", l), hT[l][:, :, 1:T + 1])
                for l in NL:
                    src = full(act, ("gv", l), i)[:, 0].rearrange("p (c n) -> p c n", c=KC)
                    fn(GV[l], src, ACT.Copy).then_inc(drain_sem(("gv", l), i), 1)
                for l in NL:
                    copy_out(("hT1", l), hT[l][:, :, 1:T + 1])
                for l in NL:
                    src = full(act, ("r", l), i)
                    fn(w3[l][:], src, ACT.Sigmoid).then_inc(drain_sem(("r", l), i), 1)
                for l in NL:
                    src = full(act, ("k", l), i)
                    ka = s[l][:].rearrange("p t d -> p (t d)").rearrange("p (c n) -> p c n", c=KC)
                    fn(ka, src, ACT.Relu).then_inc(drain_sem(("k", l), i), 1)
                    copied(act, ("k", l), i)
                    fn(ka, ka, ACT.Square).then_inc(relu_sq[l], 1)
                for l in NL:
                    copy_out(("hT2", l), hT[l][:, :, 1:T + 1])
                for stage, j, dst in (("it", 2, 0), ("rt", 3, 2)):
                    for l in NL:
                        src = full(act, (stage, l), i)
                        for dc in range(KC):
                            ins = fn(w12[l][:, dst + dc, :], src[:, dc, :], ACT.Sigmoid,
                                     bias=cols[:, j, dc:dc + 1])
                        ins.then_inc(drain_sem((stage, l), i), 1)
                for l in NL:
                    copied(act, ("rt", l), i)
                    fn(w3[l][:], xk[l], ACT.Exp, scale=cap[:, 7:8]).then_inc(a2_ready[l], 1)
                    act.wait_ge(a2_ready[l], i + 1)
                    fn(xk[l], xk[l], ACT.Exp, scale=cap[:, 4:5]).then_inc(at_ready[l], 1)
                for l in NL:
                    act.wait_ge(a2_capped[l], i + 1)
                    fn(w3[l][:], w3[l][:], ACT.Sqrt, scale=-1.0, bias=1.0).then_inc(sq_ready[l], 1)
                for l in NL:
                    copy_out(("hT3", l), hT[l][:, :, 1:T + 1])
                for l in NL:
                    for half_ in range(2):
                        src = full(act, (f"qkT{half_}", l), i)
                        if l == 1 and half_ == 0:
                            act.wait_ge(parts_stored[0], 32 * i + 32)
                        fn(qkhi[:, 2 * half_:2 * half_ + 2, :], src, ACT.Copy).then_inc(hi_ready, 1)
                n = 0
                for key, _ in attention_order():
                    if key[0] == "exp":
                        src = full(act, key, i)
                        fn(probs[n % 4], src, ACT.Exp, scale=HD ** -0.5).then_inc(drain_sem(key, i), 1)
                        n += 1
                    elif key[0] == "av":
                        _, l, g = key
                        full(act, key, i)
                        fn(num[l][:, g % 2, :], ps[:, slot_of(key, i) + SLOTS, :], ACT.Copy).then_inc(drain_sem(key, i), 1)
                        copied(act, key, i)
                        act.sem_inc(av_copied[l], 1)
                for l in NL:
                    copy_out(("aoT", l), aoT[l])
                for l in NL:
                    copy_out(("xT1", l), hT[l][:, :, 1:T + 1])
                for l in NL:
                    act.wait_ge(gate_in[l], i + 1)
                    fn(gl[l][:, 1], gl[l][:, 0], ACT.Exp).then_inc(gate_exp[l], 1)

        @block.vector
        def _(dve):
            v = nc.vector
            setup = Count(dve_own)
            dve.sem_inc(dve_setup, 1)
            for l in NL:
                v.memset(hT[l][:, :, 0:1], 0.0)
                v.memset(vp[l][:], 1.0)
            v.memset(qst[:].bitcast(F32), 0.0)
            for e in range(2):
                v.memset(kst[64 * e:64 * e + 64, :, e:4:2, :].bitcast(F32), 1.0)
                v.memset(kst[64 * e:64 * e + 64, :, 1 - e:4:2, :].bitcast(F32), 0.0)
            v.memset(ones[:], 1.0)
            v.memset(half[:], -0.5)
            setup.link(dve, v.memset(run[:], 0.0))
            dve.wait_ge(w_loaded, 16 * N_LOADS)
            setup.link(dve, v.tensor_scalar(cap[:, 5:6], cap[:, 0:1], -1.0, None, ALU.mult))
            v.tensor_tensor(cap[:, 1:2], cap[:, 0:1], cap[:, 5:6], ALU.max).then_inc(dve_setup, 1)
            setup.link(dve, v.tensor_scalar(ncols[:, 0:2], cols[:, 0:2], -1.0, 1.0, ALU.mult, ALU.add))
            setup.link(dve, v.tensor_scalar(ncols[:, 2:4], cols[:, 2:4], -1.0, None, ALU.mult))
            for m in MATS:
                src = full(dve, ("wT", m), None)[:, :, 0:D]
                dst = wT0[:, mat(m)] if mat(m) < SETUP_MATS else wT[:, mat(m) - SETUP_MATS]
                v.tensor_copy(dst, src).then_inc(drain_sem(("wT", m), None), 1)
            copied(dve, ("wT", MATS[-1]), None)
            for k in range(2 * DP):
                setup.link(dve, v.tensor_tensor(wc[:, k, :], wT0[:, mat("ws"), k % 2, :], wb[:, :, k // 2], ALU.mult))
            src = full(dve, ("at",), None)[:, 0].rearrange("p (c n) -> p c n", c=KC)
            v.tensor_scalar(at16[:], src, D ** 0.5, None, ALU.mult).then_inc(drain_sem(("at",), None), 1)
            copied(dve, ("at",), None)
            dve.wait_ge(act_setup, 2)
            setup.link(dve, v.tensor_scalar(cap[:, 5:6], cap[:, 0:1], 0.0, None, ALU.max))
            setup.link(dve, v.tensor_tensor(cap[:, 6:7], cap[:, 5:6], cap[:, 3:4], ALU.add))
            v.tensor_scalar(cap[:, 7:8], cap[:, 6:7], -16.0, None, ALU.mult)
            v.tensor_scalar(cap[:, 4:5], cap[:, 6:7], -8.0, None, ALU.mult).then_inc(dve_setup, 1)

            with dve.Fori(0, ITERS) as i:
                own = Count(dve_own, i * DVE_LINKS + setup.n)

                def link(ins):
                    own.link(dve, ins)

                def moments(l, src):
                    for tt in range(TT):
                        ins = v.bn_stats(stats[l][:, tt, :], src[:, tt, :])
                    link(ins)
                    dve.sem_inc(settled, 1)
                    for tt in range(TT):
                        ins = v.bn_aggr(mv[l][:, tt, :], stats[l][:, tt, :])
                    link(ins)
                    v.tensor_scalar(ve[l][:], mv[l][:, :, 1], EPS, None, ALU.add).then_inc(var_ready[l], 1)

                def normalise(l, src, n, dst):
                    dve.wait_ge(rstd_ready[l], NORMS * i + n + 1)
                    for tt in range(TT):
                        ins = v.tensor_scalar(dst[:, tt, :], src[:, tt, :], mv[l][:, tt, 0:1], rstd[l][:, tt:tt + 1],
                                              ALU.subtract, ALU.mult)
                    return ins

                for l in NL:
                    for tt in range(1, TT, 2):
                        src = full(dve, ("xT", l, tt), i)
                        v.tensor_copy(pt[:, tt % 2].rearrange("p (a n) -> p a n", a=2), src
                                      ).then_inc(drain_sem(("xT", l, tt), i), 1)
                for l in NL:
                    src = full(dve, ("g", l), i)[:, 0].rearrange("p (c n) -> p c n", c=KC)
                    v.tensor_copy(G[l], src).then_inc(drain_sem(("g", l), i), 1)
                for l in NL:
                    src = full(dve, ("b", l), i)[:, 0].rearrange("p (c n) -> p c n", c=KC)
                    v.tensor_copy(BM[l], src).then_inc(drain_sem(("b", l), i), 1)
                for l in NL:
                    src = by_token(full(dve, ("y", l), i))
                    dve.wait_ge(h_ready[l][0], i + 1)
                    v.tensor_tensor(s[l][:], src, h[l][:], ALU.add).then_inc(drain_sem(("y", l), i), 1)
                    copied(dve, ("y", l), i)
                    moments(l, s[l])
                for l in NL:
                    normalise(l, s[l], 0, h[l]).then_inc(h_ready[l][1], 1)

                for l in NL:
                    copied(dve, ("hT1", l), i)
                    for j, dst in ((0, xr[l]), (1, xk[l])):
                        for dc in range(KC):
                            ins = v.tensor_scalar(dst[:, dc, :], hT[l][:, dc, 1:T + 1], cols[:, j, dc:dc + 1], None, ALU.mult)
                        link(ins)
                        for dc in range(KC):
                            ins = v.scalar_tensor_tensor(out=dst[:, dc, :], in0=hT[l][:, dc, 0:T],
                                                         scalar=ncols[:, j, dc:dc + 1], in1=dst[:, dc, :],
                                                         op0=ALU.mult, op1=ALU.add)
                        ins.then_inc(mix_ready[l], 1)
                for l in NL:
                    copied(dve, ("r", l), i)
                    src = by_token(full(dve, ("kv", l), i))
                    v.tensor_tensor(s[l][:], src, by_token(w3[l]), ALU.mult).then_inc(drain_sem(("kv", l), i), 1)
                    copied(dve, ("kv", l), i)
                    dve.wait_ge(h_ready[l][1], i + 1)
                    link(v.tensor_tensor(s[l][:], s[l][:], h[l][:], ALU.add))
                    moments(l, s[l])
                for l in NL:
                    normalise(l, s[l], 1, h[l]).then_inc(h_ready[l][2], 1)

                for l in NL:
                    copied(dve, ("it", l), i)
                    copied(dve, ("hT2", l), i)
                    link(v.tensor_tensor(xr[l], xr[l], hT[l][:, :, 1:T + 1], ALU.mult))
                for l in NL:
                    dve.wait_ge(a2_ready[l], i + 1)
                    v.tensor_scalar(w3[l][:], w3[l][:], 1.0, None, ALU.min).then_inc(a2_capped[l], 1)
                for l in NL:
                    dve.wait_ge(sq_ready[l], i + 1)
                    dve.wait_ge(at_ready[l], i + 1)
                    link(v.tensor_tensor(xr[l], xr[l], w3[l][:], ALU.mult))
                    for dc in range(KC):
                        ins = v.tensor_tensor_scan(w3[l][:, dc, :], xk[l][:, dc, :], xr[l][:, dc, :], 0.0, ALU.mult, ALU.add)
                    link(ins)
                    v.tensor_tensor(w3[l][:], w3[l][:], hT[l][:, :, 1:T + 1], ALU.add).then_inc(sT_ready[l], 1)
                for l in NL:
                    src = by_token(full(dve, ("back", l), i))
                    moments(l, src)
                for l in NL:
                    ins = normalise(l, by_token(granule(slot_of(("back", l), i))), 2, h[l])
                    link(ins)
                    dve.sem_inc(drain_sem(("back", l), i), 1)
                    dve.sem_inc(h_ready[l][3], 1)

                for half_ in range(2):
                    for l in NL:
                        src = full(dve, (f"qk{half_}", l), i)
                        v.tensor_tensor(w12[l][:, 2 * half_:2 * half_ + 2, :], src,
                                        bqk[:].unsqueeze(1).to_broadcast([P, 2, 2 * D]), ALU.add
                                        ).then_inc(drain_sem((f"qk{half_}", l), i), 1)
                        copied(dve, (f"qk{half_}", l), i)
                        if half_ == 1:
                            dve.sem_inc(qkb_ready[l], 1)
                for l in NL:
                    src = by_token(full(dve, ("v", l), i)).rearrange("p t (h d) -> p t h d", d=HD)
                    bias = bv[:].rearrange("p (h d) -> p h d", d=HD).unsqueeze(1).to_broadcast([P, TT, H, HD])
                    link(v.tensor_tensor(vp[l][:, :, :, 0:HD], src, bias, ALU.add))
                    dve.sem_inc(drain_sem(("v", l), i), 1)
                    dve.sem_inc(v_ready[l], 1)
                for l in NL:
                    dve.wait_ge(swapped[l], i + 1)
                    qk = w12[l][:].rearrange("p t (h d) -> p t h d", d=HD)
                    cos = rope[:, 0].unsqueeze(2).to_broadcast([P, TT, 2 * H, HD])
                    link(v.tensor_tensor(qk, qk, cos, ALU.mult))
                    v.tensor_tensor(w12[l][:, 0:2, :], w12[l][:, 0:2, :], w3[l][:], ALU.add)
                    v.tensor_tensor(w12[l][:, 2:4, :], w12[l][:, 2:4, :],
                                    s[l][:].rearrange("p t d -> p (t d)").rearrange("p (a n) -> p a n", a=2), ALU.add
                                    ).then_inc(qk_ready[l], 1)
                for l in NL:
                    for half_ in range(2):
                        src = full(dve, (f"qkT{half_}", l), i)
                        c0 = 2 * half_
                        if l == 1 and half_ == 0:
                            dve.wait_ge(parts_stored[0], 32 * i + 32)
                        dve.wait_ge(hi_ready, 4 * i + 2 * l + half_ + 1)
                        link(v.tensor_tensor(qklo[:, c0:c0 + 2, :], src, qkhi[:, c0:c0 + 2, :].bitcast(F32), ALU.subtract))
                        dve.sem_inc(drain_sem((f"qkT{half_}", l), i), 1)
                        dve.sem_inc(lo_ready, 1)

                for key, _ in attention_order():
                    kind, l, g = key[:3]
                    gn = i * LANES * GROUPS + l * GROUPS + g
                    if kind == "max":
                        head, qh = key[3] // 2, key[3] % 2
                        src = full(dve, key, i)
                        v.tensor_reduce(mx[:, g % 2, 2 * qh:2 * qh + 2, head], src, AX_X, ALU.max
                                        ).then_inc(drain_sem(key, i), 1)
                    elif kind == "maxT":
                        src = full(dve, key, i)[0:4, 0, :]
                        dve.wait_ge(mx_stored, 16 * gn + 16)
                        link(v.tensor_scalar(mhl[:, 0, :], src, -1.0, None, ALU.mult))
                        link(v.scalar_tensor_tensor(out=mhl[:, 1, :], in0=src, scalar=-1.0, in1=mhl[:, 0, :].bitcast(F32),
                                                    op0=ALU.mult, op1=ALU.subtract))
                        dve.sem_inc(drain_sem(key, i), 1)
                        dve.sem_inc(mhl_ready, 1)
                    elif kind == "avT":
                        src = full(dve, key, i)[:, 0].rearrange("p (t h c) -> p t h c", t=TT, h=4)
                        link(v.reciprocal(rden[l][:], src[:, :, :, HD]))
                        v.tensor_tensor(ao[l].rearrange("p t (h d) -> p t h d", d=HD)[:, :, 4 * g:4 * g + 4, :], src[:, :, :, 0:HD],
                                        rden[l][:].unsqueeze(3).to_broadcast([P, TT, 4, HD]), ALU.mult
                                        ).then_inc(drain_sem(key, i), 1)
                        copied(dve, key, i)
                        dve.sem_inc(ao_ready[l], 1)
                for l in NL:
                    src = by_token(full(dve, ("wo", l), i))
                    dve.wait_ge(bo_added[l], i + 1)
                    v.tensor_tensor(s[l][:], src, h[l][:], ALU.add).then_inc(drain_sem(("wo", l), i), 1)
                    copied(dve, ("wo", l), i)
                    moments(l, s[l])
                for l in NL:
                    link(normalise(l, s[l], 3, s[l]))
                    link(v.tensor_tensor(s[l][:], s[l][:], g1t[:].unsqueeze(1).to_broadcast([P, TT, D]), ALU.mult))
                    dve.wait_ge(h3_stored[l], 16 * (i + 1))
                    v.tensor_tensor(h[l][:], s[l][:], be1t[:].unsqueeze(1).to_broadcast([P, TT, D]), ALU.add
                                    ).then_inc(h_ready[l][4], 1)

                for l in NL:
                    src = flat(full(dve, ("gate", l), i))[:, 0:TT * E].rearrange("p (t e) -> p t e", e=E)
                    lg = gl[l][:, 0]

                    def wide(ap):
                        return ap.unsqueeze(2).to_broadcast([P, TT, E])

                    v.tensor_tensor(lg, src, bg[:].unsqueeze(1).to_broadcast([P, TT, E]), ALU.add
                                    ).then_inc(drain_sem(("gate", l), i), 1)
                    copied(dve, ("gate", l), i)
                    link(v.tensor_reduce(gm[l][:, 0, :], lg, AX_X, ALU.max))
                    v.tensor_tensor(lg, lg, wide(gm[l][:, 0, :]), ALU.subtract).then_inc(gate_in[l], 1)
                for l in NL:
                    ex = gl[l][:, 1]
                    dve.wait_ge(gate_exp[l], i + 1)
                    link(v.tensor_reduce(gm[l][:, 1, :], ex, AX_X, ALU.add))
                    link(v.reciprocal(gm[l][:, 1, :], gm[l][:, 1, :]))
                    link(v.tensor_tensor(ex, ex, wide(gm[l][:, 1, :]), ALU.mult))
                    dve.sem_inc(settled, 1)
                    for tt in range(TT):
                        ins = v.max(top8[l][:, tt, :], ex[:, tt, :])
                    link(ins)
                    dve.sem_inc(settled, 1)
                    for tt in range(TT):
                        ins = v.max_index(idx8[l][:, tt, :], top8[l][:, tt, :], ex[:, tt, :])
                    link(ins)
                    link(v.tensor_tensor(gm[l][:, 2, :], top8[l][:, :, 0], top8[l][:, :, 1], ALU.add))
                    link(v.reciprocal(gm[l][:, 2, :], gm[l][:, 2, :]))
                    v.tensor_tensor(topw_all[:, bass.ds((i * LANES + l) * TT, TT), :], top8[l][:, :, 0:2],
                                    gm[l][:, 2, :].unsqueeze(2).to_broadcast([P, TT, 2]), ALU.mult)
                    link(v.tensor_copy(idxf[l][:], idx8[l][:, :, 0:2]))
                    for k in range(2):
                        ins = v.tensor_tensor(gl[l][:, 3 + k], iota8[:].unsqueeze(1).to_broadcast([P, TT, E]),
                                              wide(idxf[l][:, :, k]), ALU.is_equal)
                    link(ins)
                    v.tensor_tensor(gl[l][:, 2], gl[l][:, 3], gl[l][:, 4], ALU.add).then_inc(mask_ready[l], 1)
                for l in NL:
                    src = flat(full(dve, ("rank", l), i))
                    ranks = src[:, 0:TT * E].rearrange("p (t e) -> p t e", e=E)
                    totals = src[:, TT * E:2 * TT * E].rearrange("p (t e) -> p t e", e=E)
                    base = gl[l][:, 5]
                    link(v.tensor_tensor(base[:, 0, :], run[:], region[:], ALU.add))
                    for tt in range(1, TT):
                        link(v.tensor_tensor(base[:, tt, :], base[:, tt - 1, :], totals[:, tt - 1, :], ALU.add))
                    for tt in range(TT):
                        link(v.tensor_tensor(run[:], run[:], totals[:, tt, :], ALU.add))
                    link(v.tensor_tensor(base, base, ranks, ALU.add))
                    dve.sem_inc(drain_sem(("rank", l), i), 1)
                    for k in range(2):
                        link(v.tensor_tensor(gl[l][:, 3 + k], gl[l][:, 3 + k], base, ALU.mult))
                        link(v.tensor_reduce(gm[l][:, 2 + k, :], gl[l][:, 3 + k], AX_X, ALU.add))
                    dve.wait_ge(rows_away[l], i + 1)
                    for k in range(2):
                        v.tensor_copy(slot_i[l][:, :, k], gm[l][:, 2 + k, :])
                        ins = v.tensor_copy(slots_all[:, bass.ds((i * LANES + l) * TT, TT), k], gm[l][:, 2 + k, :])
                    link(ins)
                    dve.sem_inc(slot_ready[l], 1)
                assert own.n == DVE_LINKS, own.n

        @block.gpsimd
        def _(pool):
            q = nc.gpsimd
            q.memset(ident[:], 0.0).then_inc(pool_setup, 1)
            pool.wait_ge(pool_setup, 1)
            q.affine_select(out=ident[:], in_=ident[:], compare_op=ALU.not_equal, fill=1.0, base=0,
                            pattern=[[-1, P]], channel_multiplier=1).then_inc(pool_setup, 1)
            q.memset(ntri[:], 1.0).then_inc(pool_setup, 1)
            pool.wait_ge(pool_setup, 3)
            q.affine_select(out=ntri[:], in_=ntri[:], compare_op=ALU.is_gt, fill=0.0, base=0,
                            pattern=[[1, P]], channel_multiplier=-1)
            q.iota(iota8[:], pattern=[[1, E]], base=0, channel_multiplier=0, allow_small_or_imprecise_dtypes=True)
            q.iota(region[:], pattern=[[REGION, E]], base=0, channel_multiplier=0,
                   allow_small_or_imprecise_dtypes=True).then_inc(pool_setup, 1)
            for sem_ in drained + x_used + rows_away + st_used:
                pool.sem_inc(sem_, 1)
            for sem_ in x1_stored + [mx_stored]:
                pool.sem_inc(sem_, 16)
            pool.wait_ge(dve_own, 1)
            pool.wait_ge(w_loaded, 16 * N_LOADS)

            with pool.Fori(0, ITERS) as i:
                def rsqrt(n):
                    for l in NL:
                        pool.wait_ge(var_ready[l], NORMS * i + n + 1)
                        q.tensor_tensor(rstd[l][:], ve[l][:], half[:], ALU.pow).then_inc(rstd_ready[l], 1)

                for n in range(3):
                    rsqrt(n)
                for l in NL:
                    pool.wait_ge(qkb_ready[l], i + 1)
                    for tt in range(TT):
                        x_ = w12[l][:, tt, :].rearrange("p (h d) -> p h d", d=HD)
                        y_ = (w3[l][:, tt, :] if tt < 2 else
                              s[l][:].rearrange("p t d -> p (t d)")[:, (tt - 2) * T:(tt - 1) * T]).rearrange("p (h d) -> p h d", d=HD)
                        for half_ in range(2):
                            a_, b_ = half_ * HD // 2, (1 - half_) * HD // 2
                            sin = rope[:, 1, tt, a_:a_ + HD // 2].unsqueeze(1).to_broadcast([P, 2 * H, HD // 2])
                            ins = q.tensor_tensor(y_[:, :, a_:a_ + HD // 2], x_[:, :, b_:b_ + HD // 2], sin, ALU.mult)
                    ins.then_inc(swapped[l], 1)
                for l in NL:
                    pool.wait_ge(h3_stored[l], 16 * (i + 1))
                    full(pool, ("hT3", l), i)
                    q.tensor_tensor(h[l][:], h[l][:], bo[:].unsqueeze(1).to_broadcast([P, TT, D]), ALU.add).then_inc(bo_added[l], 1)
                rsqrt(3)
                for l in NL:
                    pool.wait_ge(slot_ready[l], i + 1)
                    pool.sem_inc(settled_pool, 1)
                    for tt in range(TT):
                        for k in range(2):
                            q.indirect_dma_start(xs[:], bass.IndirectOffsetOnAxis(ap=slot_i[l][:, tt, k:k + 1], axis=0),
                                                 h[l][:, tt, :], None).then_inc(scattered[l], 16)
                for l in NL:
                    pool.wait_ge(scattered[l], 16 * 2 * TT * (i + 1))
                    pool.sem_inc(rows_away[l], 1)
        p1.close()

        NJ = range(2)
        w1 = sbuf(ctx, "w1", [P, E, KC, FF])
        w2 = sbuf(ctx, "w2", [P, E, FC, D])
        b1 = sbuf(ctx, "b1", [P, E, FF])
        b2 = sbuf(ctx, "b2", [P, E, D])
        p2 = ctx.enter_context(ExitStack())
        zeros = sbuf(p2, "zeros", [P, D])
        steps = sbuf(p2, "steps", [P, STEPS, 2], I32)
        ends = sbuf(p2, "ends", [P, 2, E])
        pad = sbuf(p2, "pad", [P, E], I32)
        many = sbuf(p2, "many", [P, E, B * T // P])
        edge = sbuf(p2, "edge", [P, B * T // P])
        step_no = sbuf(p2, "step_no", [P, STEPS])
        past = sbuf(p2, "past", [P, STEPS, E])
        tmp = sbuf(p2, "tmp", [P, 4, STEPS])
        first = sbuf(p2, "first", [P, E])
        pad_f = sbuf(p2, "pad_f", [P, E])
        slot_f = sbuf(p2, "slot_f", [P, 2 * TILES])
        spare = sbuf(p2, "spare", [P, E - 1])
        beyond = sbuf(p2, "beyond", [P, 2 * TILES, E - 1])
        moved = sbuf(p2, "moved", [P, 2 * TILES])
        xrow = [sbuf(p2, f"xrow{j}", [P, D]) for j in NJ]
        xTe = [sbuf(p2, f"xTe{j}", [P, KC, P]) for j in NJ]
        he = [sbuf(p2, f"he{j}", [P, FF]) for j in NJ]
        heT = [sbuf(p2, f"heT{j}", [P, FC, P]) for j in NJ]
        ye = [sbuf(p2, f"ye{j}", [P, D]) for j in NJ]

        table_ready, setup2 = sem("steps_ready"), sem("phase2_setup")
        experts_loaded, biases_loaded, padded = sem("experts_loaded"), sem("biases_loaded"), sem("padded")
        rows_loaded, rows_turned, rowsT_ready = sems("rows_loaded", 2), sem("rows_turned"), sem("rowsT_ready")
        l1_done, l1_biased, gelu_done = sem("l1_done"), sem("l1_biased"), sem("gelu_done")
        h_turned, hT_act, hT_dve = sem("hidden_turned"), sem("hiddenT_act"), sem("hiddenT_dve")
        l2_done, l2_biased, y_stored = sem("l2_done"), sem("l2_biased"), sems("y_stored", 2)
        own2 = sem("dve_own2")

        def at_least(eng, sem_, value):
            if not isinstance(value, int) or value > 0:
                eng.wait_ge(sem_, value)

        def pipeline(eng, lag, body):
            for n in range(4):
                body(n, n % 2)
            with eng.Fori(0, (STEPS - 6) // 2) as it:
                for j in NJ:
                    body(it * 2 + 4 + j, j)
            for n in range(STEPS - 2, STEPS + lag):
                body(n, n % 2)

        def inside(n, lag):
            return not isinstance(n, int) or 0 <= n - lag < STEPS

        blk = ctx.enter_context(ExitStack())
        block2 = blk.enter_context(nc.Block())
        pX = ps[:, 0, 0:KC * P]
        pY = ps[:, 1, 0:D]
        pH = [ps[:, 2:4, :], ps[:, 4:6, :]]
        pT = ps[:, 6:8, :]

        @block2.sync
        def _(sp):
            sp.wait_ge(table_ready, 1)
            for e in range(E):
                row = sp.value_load(pad[0:1, e:e + 1], min_val=0, max_val=ROWS - P)
                sp.dma_start(xs[bass.ds(row, P), :], zeros[:]).then_inc(padded, 16)
            for e in range(E):
                sp.dma_start(xs[E * REGION + e * P:E * REGION + (e + 1) * P, :], zeros[:]).then_inc(padded, 16)
            sp.wait_ge(padded, 16 * 2 * E)

            def body(n, j):
                if inside(n, 0):
                    row = sp.value_load(steps[0:1, bass.ds(n, 1), 1], min_val=0, max_val=ROWS - P)
                    at_least(sp, rows_turned, n - 1)
                    sp.dma_start(xrow[j][:], xs[bass.ds(row, P), :]).then_inc(rows_loaded[j], 16)
                if inside(n, 4):
                    sp.wait_ge(l2_biased, n - 3)
                    sp.dma_start(ys.rearrange("(s p) d -> s p d", p=P)[bass.ds(n - 4, 1)].rearrange("o p d -> (o p) d"), ye[j][:]).then_inc(y_stored[j], 16)

            pipeline(sp, 4, body)
            for j in NJ:
                sp.wait_ge(y_stored[j], 16 * STEPS // 2)

        @block2.tensor
        def _(pe):
            mm, tr = nc.tensor.matmul, nc.tensor.transpose
            pe.wait_ge(table_ready, 1)

            def turn_rows(n, j):
                pe.wait_ge(rows_loaded[j], 16 * ((n - j) // 2 + 1) if isinstance(n, int) else 8 * (n - j) + 16)
                at_least(pe, rowsT_ready, n)
                for kc in range(KC):
                    ins = tr(pX[:, kc * P:(kc + 1) * P], xrow[j][:, kc * P:(kc + 1) * P], ident[:])
                ins.then_inc(rows_turned, 1)

            def body(n, j):
                if isinstance(n, int) and n == 0:
                    turn_rows(0, 0)
                if inside(n, 0):
                    e = pe.value_load(steps[0:1, bass.ds(n, 1), 0], min_val=0, max_val=E - 1)
                    pe.wait_ge(rowsT_ready, n + 1)
                    at_least(pe, l1_biased, n - 1)
                    pe.wait_ge(experts_loaded, e * 32 + 32)
                    for c in range(2):
                        for kc in range(KC):
                            ins = mm(pH[j][:, c, :], xTe[j][:, kc, :],
                                     w1[:, bass.ds(e, 1), kc, c * 512:(c + 1) * 512].rearrange("p o n -> p (o n)"),
                                     start=kc == 0, stop=kc == KC - 1)
                    ins.then_inc(l1_done, 1)
                if inside(n, -1):
                    turn_rows(n + 1, 1 - j)
                if inside(n, 1):
                    pe.wait_ge(gelu_done, n)
                    at_least(pe, hT_act, n - 1)
                    at_least(pe, hT_dve, n - 1)
                    for f in range(FC):
                        ins = tr(pT[:, f // 4, (f % 4) * P:(f % 4 + 1) * P], he[1 - j][:, f * P:(f + 1) * P], ident[:])
                    ins.then_inc(h_turned, 1)
                if inside(n, 2):
                    e = pe.value_load(steps[0:1, bass.ds(n - 2, 1), 0], min_val=0, max_val=E - 1)
                    pe.wait_ge(hT_act, n - 1)
                    pe.wait_ge(hT_dve, n - 1)
                    at_least(pe, l2_biased, n - 2)
                    for f in range(FC):
                        ins = mm(pY, heT[j][:, f, :],
                                 w2[:, bass.ds(e, 1), f, :].rearrange("p o n -> p (o n)"),
                                 start=f == 0, stop=f == FC - 1)
                    ins.then_inc(l2_done, 1)

            pipeline(pe, 2, body)

        @block2.scalar
        def _(act):
            fn = nc.scalar.activation

            def turned(n, j):
                act.wait_ge(rows_turned, n + 1)
                at_least(act, l1_done, n - 1)
                fn(xTe[j][:], pX.rearrange("p (c t) -> p c t", c=KC), ACT.Copy).then_inc(rowsT_ready, 1)

            def body(n, j):
                if isinstance(n, int) and n == 0:
                    turned(0, 0)
                if inside(n, -1):
                    turned(n + 1, 1 - j)
                if inside(n, 1):
                    act.wait_ge(h_turned, n)
                    at_least(act, l2_done, n - 2)
                    fn(heT[1 - j][:, 0:4, :], pT[:, 0, :].rearrange("p (f t) -> p f t", t=P), ACT.Copy).then_inc(hT_act, 1)
                if inside(n, 0):
                    act.wait_ge(l1_biased, n + 1)
                    fn(he[j][:], he[j][:], ACT.Gelu).then_inc(gelu_done, 1)

            pipeline(act, 1, body)

        @block2.vector
        def _(dve):
            v = nc.vector
            own = Count(own2)

            def link(ins):
                own.link(dve, ins)

            link(v.memset(zeros[:], 0.0))
            dve.wait_ge(setup2, 1)
            counts = run[:].unsqueeze(2).to_broadcast([P, E, B * T // P])
            link(v.tensor_tensor(many[:], counts, edge[:].unsqueeze(1).to_broadcast([P, E, B * T // P]), ALU.is_gt))
            link(v.tensor_reduce(ends[:, 0, :], many[:], AX_X, ALU.add))
            link(v.tensor_copy(ends[:, 1, 0:1], ends[:, 0, 0:1]))
            for e in range(1, E):
                link(v.tensor_tensor(ends[:, 1, e:e + 1], ends[:, 1, e - 1:e], ends[:, 0, e:e + 1], ALU.add))
            link(v.tensor_tensor(past[:], step_no[:].unsqueeze(2).to_broadcast([P, STEPS, E]),
                                 ends[:, 1, :].unsqueeze(1).to_broadcast([P, STEPS, E]), ALU.is_ge))
            link(v.tensor_reduce(tmp[:, 0, :], past[:], AX_X, ALU.add))
            link(v.tensor_tensor(past[:], past[:], ends[:, 0, :].unsqueeze(1).to_broadcast([P, STEPS, E]), ALU.mult))
            link(v.tensor_reduce(tmp[:, 1, :], past[:], AX_X, ALU.add))
            link(v.tensor_tensor(tmp[:, 1, :], step_no[:], tmp[:, 1, :], ALU.subtract))
            link(v.tensor_scalar(tmp[:, 1, :], tmp[:, 1, :], float(P), None, ALU.mult))
            link(v.tensor_scalar(tmp[:, 2, :], tmp[:, 0, :], float(REGION), None, ALU.mult))
            link(v.tensor_tensor(tmp[:, 1, :], tmp[:, 1, :], tmp[:, 2, :], ALU.add))
            link(v.tensor_scalar(tmp[:, 0, :], tmp[:, 0, :], float(E - 1), None, ALU.min))
            v.tensor_copy(steps[:, :, 0], tmp[:, 0, :])
            v.tensor_copy(steps[:, :, 1], tmp[:, 1, :])
            link(v.tensor_tensor(pad_f[:], first[:], run[:], ALU.add))
            v.tensor_copy(pad[:], pad_f[:]).then_inc(table_ready, 1)
            dve.wait_ge(table_ready, 1)
            link(v.tensor_scalar(spare[:], ends[:, 0, 0:E - 1], float(P), float(-REGION), ALU.mult, ALU.add))
            link(v.tensor_copy(slot_f[:], flat(slots_all[:])))
            link(v.tensor_tensor(beyond[:], slot_f[:].unsqueeze(2).to_broadcast([P, 2 * TILES, E - 1]),
                                 first[:, 1:E].unsqueeze(1).to_broadcast([P, 2 * TILES, E - 1]), ALU.is_ge))
            link(v.tensor_tensor(beyond[:], beyond[:], spare[:].unsqueeze(1).to_broadcast([P, 2 * TILES, E - 1]), ALU.mult))
            link(v.tensor_reduce(moved[:], beyond[:], AX_X, ALU.add))
            link(v.tensor_tensor(slot_f[:], slot_f[:], moved[:], ALU.add))
            link(v.tensor_copy(flat(slots_all[:]), slot_f[:]))
            dve.wait_ge(biases_loaded, 64)

            def body(n, j):
                if inside(n, 0):
                    e = dve.value_load(steps[0:1, bass.ds(n, 1), 0], min_val=0, max_val=E - 1)
                    dve.wait_ge(l1_done, n + 1)
                    at_least(dve, h_turned, n - 1)
                    v.tensor_tensor(he[j][:], pH[j].rearrange("p a n -> p (a n)"),
                                    b1[:, bass.ds(e, 1), :].rearrange("p o n -> p (o n)"), ALU.add).then_inc(l1_biased, 1)
                if inside(n, 1):
                    dve.wait_ge(h_turned, n)
                    at_least(dve, l2_done, n - 2)
                    v.tensor_copy(heT[1 - j][:, 4:8, :], pT[:, 1, :].rearrange("p (f t) -> p f t", t=P)).then_inc(hT_dve, 1)
                if inside(n, 2):
                    e = dve.value_load(steps[0:1, bass.ds(n - 2, 1), 0], min_val=0, max_val=E - 1)
                    dve.wait_ge(l2_done, n - 1)
                    at_least(dve, y_stored[j], 16 * ((n - 2) // 2) if isinstance(n, int) else 8 * (n - j) - 16)
                    v.tensor_tensor(ye[j][:], pY, b2[:, bass.ds(e, 1), :].rearrange("p o n -> p (o n)"),
                                    ALU.add).then_inc(l2_biased, 1)

            pipeline(dve, 2, body)

        @block2.gpsimd
        def _(pool):
            q = nc.gpsimd
            q.iota(edge[:], pattern=[[P, B * T // P]], base=0, channel_multiplier=0, allow_small_or_imprecise_dtypes=True)
            q.iota(step_no[:], pattern=[[1, STEPS]], base=0, channel_multiplier=0, allow_small_or_imprecise_dtypes=True)
            q.iota(first[:], pattern=[[REGION, E]], base=0, channel_multiplier=0,
                   allow_small_or_imprecise_dtypes=True).then_inc(setup2, 1)
            for e in range(E):
                q.dma_start(w1[:, e], a["L1_ffn_W1"][e].rearrange("(c p) n -> p c n", p=P)).then_inc(experts_loaded, 16)
                q.dma_start(w2[:, e], a["L1_ffn_W2"][e].rearrange("(c p) n -> p c n", p=P)).then_inc(experts_loaded, 16)
                if e == 0:
                    q.dma_start(b1[:].rearrange("p e n -> p (e n)"), bcast(a["L1_ffn_b1"].rearrange("e n -> (e n)"), E * FF)).then_inc(biases_loaded, 32)
                    q.dma_start(b2[:].rearrange("p e n -> p (e n)"), bcast(a["L1_ffn_b2"].rearrange("e n -> (e n)"), E * D)).then_inc(biases_loaded, 32)
                pool.wait_ge(experts_loaded, 32 * (e + 1))

        blk.close()
        p2.close()

        GRP = TILES // 2 // 2
        g2t = sbuf(ctx, "g2t", [P, D])
        be2t = sbuf(ctx, "be2t", [P, D])
        half2 = sbuf(ctx, "half2", [P, 2])
        x1b = [sbuf(ctx, f"x1b{j}", [P, 2, D]) for j in NJ]
        h3b = [sbuf(ctx, f"h3b{j}", [P, 2, D]) for j in NJ]
        yb = [sbuf(ctx, f"yb{j}", [P, 2, 2, D]) for j in NJ]
        ob = [sbuf(ctx, f"ob{j}", [P, 2, D]) for j in NJ]
        where = [sbuf(ctx, f"where{j}", [P, 2, 2], I32) for j in NJ]
        stats3 = [sbuf(ctx, f"stats3_{j}", [P, 2, 6]) for j in NJ]
        mv3 = [sbuf(ctx, f"mv3_{j}", [P, 2, 2]) for j in NJ]
        ve3 = [sbuf(ctx, f"ve3_{j}", [P, 2]) for j in NJ]
        rstd3 = [sbuf(ctx, f"rstd3_{j}", [P, 2]) for j in NJ]
        gains_loaded, half_ready, where_ready = sem("gains_loaded"), sem("half_ready"), sem("where_ready")
        x1b_loaded, h3b_loaded, yb_loaded = sems("x1b_loaded"), sems("h3b_loaded"), sems("yb_loaded")
        rows_added, h3_added = sems("rows_added"), sems("h3_added")
        var3, rstd3_ready = sems("var3_ready"), sems("rstd3_ready")
        out_ready, out_stored, own3, settled3 = sems("out_ready"), sems("out_stored"), sem("dve_own3"), sem("settled3")
        settled_p3 = sem("settled_pool3")

        blk = ctx.enter_context(ExitStack())
        block3 = blk.enter_context(nc.Block())
        tiled = lambda ap: ap.rearrange("(t p) d -> t p d", p=P)
        out_t = out.rearrange("b (t p) d -> (b t) p d", p=P)

        @block3.sync
        def _(sp):
            sp.dma_start(g2t[:], bcast(a["L1_ffn_g2"], D)).then_inc(gains_loaded, 16)
            sp.dma_start(be2t[:], bcast(a["L1_ffn_be2"], D)).then_inc(gains_loaded, 16)
            with sp.Fori(0, GRP) as i:
                for j in NJ:
                    t0 = (i * 2 + j) * 2
                    sp.wait_ge(rows_added[j], i + 1)
                    sp.dma_start(x1b[j][:], tiled(x1_all)[bass.ds(t0, 2)].rearrange("t p d -> p t d")).then_inc(x1b_loaded[j], 16)
                    sp.wait_ge(h3_added[j], i + 1)
                    sp.dma_start(h3b[j][:], tiled(h3_all)[bass.ds(t0, 2)].rearrange("t p d -> p t d")).then_inc(h3b_loaded[j], 16)
                for j in NJ:
                    t0 = (i * 2 + j) * 2
                    sp.wait_ge(out_ready[j], i + 1)
                    sp.dma_start(out_t[bass.ds(t0, 2)].rearrange("t p d -> p t d"), ob[j][:]).then_inc(out_stored[j], 16)
            for j in NJ:
                sp.wait_ge(out_stored[j], 16 * (GRP + 1))

        @block3.gpsimd
        def _(pool):
            q = nc.gpsimd
            for sem_ in rows_added + h3_added:
                pool.sem_inc(sem_, 1)
            for sem_ in out_stored:
                pool.sem_inc(sem_, 16)
            pool.wait_ge(half_ready, 1)
            with pool.Fori(0, GRP) as i:
                for j in NJ:
                    pool.wait_ge(rows_added[j], i + 1)
                    pool.sem_inc(settled_p3, 1)
                    q.tensor_copy(where[j][:], slots_all[:, bass.ds((i * 2 + j) * 2, 2), :]).then_inc(where_ready, 1)
                    pool.wait_ge(where_ready, i * 2 + j + 1)
                    pool.sem_inc(settled_p3, 1)
                    for t in range(2):
                        for k in range(2):
                            q.indirect_dma_start(yb[j][:, t, k, :], None, ys[:],
                                                 bass.IndirectOffsetOnAxis(ap=where[j][:, t, k:k + 1], axis=0)).then_inc(yb_loaded[j], 16)
                for n in range(2):
                    for j in NJ:
                        pool.wait_ge(var3[j], 2 * i + n + 1)
                        q.tensor_tensor(rstd3[j][:], ve3[j][:], half2[:], ALU.pow).then_inc(rstd3_ready[j], 1)

        @block3.vector
        def _(dve):
            v = nc.vector
            v.memset(half2[:], -0.5).then_inc(half_ready, 1)
            dve.wait_ge(gains_loaded, 32)
            with dve.Fori(0, GRP) as i:
                own = Count(own3, i * LINKS3)

                def link(ins):
                    own.link(dve, ins)

                def moments(j):
                    for t in range(2):
                        ins = v.bn_stats(stats3[j][:, t, :], ob[j][:, t, :])
                    link(ins)
                    dve.sem_inc(settled3, 1)
                    for t in range(2):
                        ins = v.bn_aggr(mv3[j][:, t, :], stats3[j][:, t, :])
                    link(ins)
                    v.tensor_scalar(ve3[j][:], mv3[j][:, :, 1], EPS, None, ALU.add).then_inc(var3[j], 1)

                def normalise(j, n):
                    dve.wait_ge(rstd3_ready[j], 2 * i + n + 1)
                    for t in range(2):
                        ins = v.tensor_scalar(ob[j][:, t, :], ob[j][:, t, :], mv3[j][:, t, 0:1], rstd3[j][:, t:t + 1],
                                              ALU.subtract, ALU.mult)
                    return ins

                for j in NJ:
                    dve.wait_ge(x1b_loaded[j], 16 * i + 16)
                    dve.wait_ge(yb_loaded[j], 64 * i + 64)
                    dve.wait_ge(out_stored[j], 16 * i + 16)
                    w = topw_all[:, bass.ds((i * 2 + j) * 2, 2), :]
                    link(v.tensor_tensor(yb[j][:], yb[j][:], w.unsqueeze(3).to_broadcast([P, 2, 2, D]), ALU.mult))
                    link(v.tensor_tensor(ob[j][:], yb[j][:, :, 0, :], yb[j][:, :, 1, :], ALU.add))
                    v.tensor_tensor(ob[j][:], ob[j][:], x1b[j][:], ALU.add).then_inc(rows_added[j], 1)
                    dve.wait_ge(rows_added[j], i + 2)
                    moments(j)
                for j in NJ:
                    link(normalise(j, 0))
                    link(v.tensor_tensor(ob[j][:], ob[j][:], g2t[:].unsqueeze(1).to_broadcast([P, 2, D]), ALU.mult))
                    link(v.tensor_tensor(ob[j][:], ob[j][:], be2t[:].unsqueeze(1).to_broadcast([P, 2, D]), ALU.add))
                    dve.wait_ge(h3b_loaded[j], 16 * i + 16)
                    v.tensor_tensor(ob[j][:], ob[j][:], h3b[j][:], ALU.add).then_inc(h3_added[j], 1)
                    dve.wait_ge(h3_added[j], i + 2)
                    moments(j)
                for j in NJ:
                    normalise(j, 1).then_inc(out_ready[j], 1)
                assert own.n == LINKS3, own.n

        blk.close()


_INS = ["x", "L0_tok_weight", "L0_tok_weighted_sum", "L0_attn_w_q", "L0_attn_w_k", "L0_attn_w_v", "L0_ffn_W_r",
        "L0_ffn_W_k", "L0_ffn_W_v", "L0_ffn_mu_r", "L0_ffn_mu_k", "L1_attn_Wi", "L1_attn_bi", "L1_attn_Wr",
        "L1_attn_br", "L1_attn_cap_lambda", "L1_ffn_Wq", "L1_ffn_bq", "L1_ffn_Wk", "L1_ffn_bk", "L1_ffn_Wv",
        "L1_ffn_bv", "L1_ffn_Wo", "L1_ffn_bo", "L1_ffn_Wg", "L1_ffn_bg", "L1_ffn_W1", "L1_ffn_b1", "L1_ffn_W2",
        "L1_ffn_b2", "L1_ffn_g1", "L1_ffn_be1", "L1_ffn_g2", "L1_ffn_be2"]


def rope_table():
    import numpy as np

    inv = (np.float32(1.0) / np.float32(10000.0) ** (np.arange(0, HD, 2, dtype=np.float32) / np.float32(HD))).astype(np.float32)
    freqs = np.arange(T, dtype=np.float32)[:, None] * inv[None, :]
    cos, sin = np.cos(freqs), np.sin(freqs)
    return np.stack([np.concatenate([cos, cos], 1), np.concatenate([-sin, sin], 1)]).astype(np.float32)


def kernel(**inputs):
    import numpy as _np
    import concourse.bacc as _bacc
    from concourse import mybir as _mybir
    from concourse.bass_utils import run_bass_kernel_spmd as _run

    nc = _bacc.Bacc("TRN2", target_bir_lowering=False, num_devices=1)
    arrays, args = {}, {}
    for name in _INS + ["rope"]:
        a = rope_table() if name == "rope" else _np.ascontiguousarray(inputs[name])
        arrays[f"in_{name}_dram"] = a
        args[name] = nc.dram_tensor(f"in_{name}_dram", a.shape, _mybir.dt.from_np(a.dtype), kind="ExternalInput").ap()
    out = nc.dram_tensor("out_0_dram", (B, T, D), F32, kind="ExternalOutput").ap()
    tower(nc, args, out)
    r = _run(nc, [arrays], core_ids=[0])
    return r.results[0]["out_0_dram"]
```

```python
from contextlib import ExitStack

import concourse.bass as bass
from concourse import mybir

F32 = mybir.dt.float32
F32R = mybir.dt.float32r
I32 = mybir.dt.int32
U32 = mybir.dt.uint32
ALU = mybir.AluOpType
ACT = mybir.ActivationFunctionType
AX_X = mybir.AxisListType.X

P = 128
B, T, D = 8, 512, 256
DP = 4
LANES = 2
ITERS = B // LANES
TT = T // P
KC = D // P
H, HD = 16, 16
E, FF = 8, 1024
FC = FF // P
TILES = B * TT
GROUPS = H // 4
EPS = 1e-5
NORMS = 4
N_LOADS = 28
DVE_LINKS = 106
MIX_FIRST = (3, 3, 1)
MIX_AFTER = (('xT1', 2), ('gate', 1), ('rank', 2))
STACK_DMAS = 14
LINKS3 = 36
REGION = B * T + P
ROWS = E * REGION + E * P
STEPS = B * T * 2 // P + E
SLOTS = 3
AV, SMALL = 3, 4
PAIR = (0, 1)
MAX = (5, 6)
ALL_SLOTS = 7
PARTS = 3
ROW_MAX = PARTS * HD
SETUP_MATS = 3
MATS = ("ws", "wq", "wk", "fr", "fk", "fv", "ai", "ar")


def psum_plan():
    def place(keys):
        at, used, out = 0, [0] * ALL_SLOTS, {}
        for key, slots in keys:
            if slots is None:
                slots = range(SLOTS)
            if key[0] == "max":
                slot = MAX[key[-1] % 2]
            elif key[0] in ("maxT", "avT"):
                slot = SMALL
            elif key[0] == "av":
                slot = AV
            else:
                slot = slots[at % len(slots)]
                at += 1
            out[key] = (slot, used[slot])
            used[slot] += 1
        return out, used

    def turn(last):
        before, attention, after = attention_order(last)
        keys = []
        for stage in ("hT0", "g", "gv", "b", "y", "hT1", "r", "k", "kv", "hT2", "rt", "it", "back", "hT3",
                      "qk0", "qk1", "v"):
            keys += [((stage, lane), None) for lane in range(LANES)]
        for lane in range(LANES):
            keys += [(key, None) for key in before[lane]] + [((f"qkT{half}", lane), None) for half in range(2)]
        keys += [(key, None) for key in before[LANES]]
        keys += [(key, PAIR) for key in attention]
        for stage in ("aoT", "wo", "xT1", "gate", "rank"):
            keys += [(key, None) for key in after.get(stage, ())]
            keys += [((stage, lane), None) for lane in range(LANES)]
        return keys

    setup = [(("wT", m), None) for m in MATS] + [(("at",), None)] + [(key, None) for key in mixing_order()]
    return place(setup), place(turn(False)), place(turn(True))


def mixing_order():
    tiles = [(lane, tt) for lane in range(LANES) for tt in range(TT)]
    out = [("xT",) + tiles[0]]
    for at, tile in enumerate(tiles):
        if at + 1 < len(tiles):
            out.append(("xT",) + tiles[at + 1])
        out.append(("tok",) + tile)
    return out


def attention_order(last):
    groups = [(lane, g) for lane in range(LANES) for g in range(GROUPS)]
    mixing = [] if last else mixing_order()
    before, out = [], []
    for n in MIX_FIRST:
        before.append(mixing[:n])
        mixing = mixing[n:]
    for step in range(len(groups) + 2):
        ahead = groups[step] if step < len(groups) else None
        now = groups[step - 2] if step >= 2 else None
        for n in range(8):
            if now:
                out.append(("exp",) + now + (n,))
            if ahead:
                out += [("max",) + ahead + (2 * n,), ("max",) + ahead + (2 * n + 1,)]
            if n == 1 and 1 <= step <= len(groups):
                out.append(("maxT",) + groups[step - 1])
            if n == 2 and step >= 3:
                out.append(("av",) + groups[step - 3])
            if n == 6 and step >= 3:
                out.append(("avT",) + groups[step - 3])
            if not now and n % 4 == 3 and mixing:
                out.append(mixing.pop(0))
    after = {}
    for stage, n in MIX_AFTER:
        after[stage], mixing = mixing[:n], mixing[n:]
    assert not mixing
    return before, out + [("av",) + groups[-1], ("avT",) + groups[-1]], after


def stacks_value(l, g, i):
    if g < 2 or l == 0:
        return min(g, 1), 16 * STACK_DMAS * (i * LANES + l + 1)
    return g, 16 * STACK_DMAS * (i + 1)


class Count:

    def __init__(self, sem, base=0):
        self.sem, self.base, self.n = sem, base, 0

    def link(self, eng, ins):
        self.n += 1
        ins.then_inc(self.sem, 1)
        eng.wait_ge(self.sem, self.base + self.n)


def tower(nc, a, out):
    with ExitStack() as ctx:
        def sem(name):
            return ctx.enter_context(nc.semaphore(name))

        def sems(name, n=LANES):
            return [sem(f"{name}{j}") for j in range(n)]

        (plan_setup, used_setup), (plan_turn, used), (plan_last, _) = psum_plan()
        ps = ctx.enter_context(nc.psum_tensor("ps", [P, 8, 512], F32))

        def granule(slot):
            if slot < SLOTS:
                return ps[:, 2 * slot:2 * slot + 2, :]
            return ps[:, 2 * SLOTS - 2 + MAX.index(slot) if slot in MAX else 2 * SLOTS + slot - AV, :]

        filled, drained = sems("psum_filled", ALL_SLOTS), sems("psum_drained", ALL_SLOTS)

        def plan_of(i):
            return plan_setup if i is None else plan_last if isinstance(i, int) else plan_turn

        def slot_of(key, i):
            return plan_of(i)[key][0]

        def fill_value(key, i):
            if i is None:
                return plan_setup[key][1] + 1
            slot, n = plan_of(i)[key]
            return used_setup[slot] + n + 1 + i * used[slot]

        def room(eng, key, i):
            slot = slot_of(key, i)
            eng.wait_ge(drained[slot], fill_value(key, i))
            return granule(slot)

        def full(eng, key, i):
            slot = slot_of(key, i)
            eng.wait_ge(filled[slot], fill_value(key, i))
            return granule(slot)

        def copied(eng, key, i):
            slot = slot_of(key, i)
            eng.wait_ge(drained[slot], fill_value(key, i) + 1)

        def fill_sem(key, i):
            return filled[slot_of(key, i)]

        def drain_sem(key, i):
            return drained[slot_of(key, i)]

        def sbuf(stack, name, shape, dt=F32):
            return stack.enter_context(nc.sbuf_tensor(name, shape, dt))

        def dram(name, shape, dt=F32):
            return nc.dram_tensor(name, shape, dt, kind="Internal").ap()

        qk_parts = dram("qk_parts", (LANES, 2, 2 * D, T))
        mx_parts = dram("mx_parts", (LANES, GROUPS, 2, 4, T))
        xs = dram("xs", (ROWS, D))
        ys = dram("ys", (STEPS * P, D))
        h3_all = dram("h3_all", (B * T, D))
        x1_all = dram("x1_all", (B * T, D))

        ident = sbuf(ctx, "ident", [P, P])
        slots_all = sbuf(ctx, "slots_all", [P, TILES, 2], I32)
        topw_all = sbuf(ctx, "topw_all", [P, TILES, 2])
        run = sbuf(ctx, "run", [P, E])

        p1 = ctx.enter_context(ExitStack())
        NL = range(LANES)
        wT = sbuf(p1, "wT", [P, len(MATS) - SETUP_MATS, KC, D])
        wc = sbuf(p1, "wc", [P, DP * 2, D])
        wv0 = sbuf(p1, "wv0", [P, KC, D])
        at16 = sbuf(p1, "at16", [P, KC, D])
        wqk = sbuf(p1, "wqk", [P, KC, 2 * D])
        wv1 = sbuf(p1, "wv1", [P, KC, D])
        wo = sbuf(p1, "wo", [P, KC, D])
        bo = sbuf(p1, "bo", [P, D])
        wg = sbuf(p1, "wg", [P, KC, E])
        bqk = sbuf(p1, "bqk", [P, 2 * D])
        bv = sbuf(p1, "bv", [P, D])
        bg = sbuf(p1, "bg", [P, E])
        g1t = sbuf(p1, "g1t", [P, D])
        be1t = sbuf(p1, "be1t", [P, D])
        rope = sbuf(p1, "rope", [P, 2, TT, HD])
        cols = sbuf(p1, "cols", [P, 4, KC])
        ncols = sbuf(p1, "ncols", [P, 2, KC])
        cap = sbuf(p1, "cap", [P, 8])
        ntri = sbuf(p1, "ntri", [P, P])
        ones = sbuf(p1, "ones", [P, P])
        region = sbuf(p1, "region", [P, E])
        iota8 = sbuf(p1, "iota8", [P, E])
        half = sbuf(p1, "half", [P, TT])
        xin = sbuf(p1, "xin", [P, TT, D * DP])
        wnat = xin[:].rearrange("p t n -> p (t n)").rearrange("p (m c n) -> p m c n", m=len(MATS), c=KC)
        pt = sbuf(p1, "pt", [P, 2, 2 * T])
        xT = [sbuf(p1, f"xT{j}", [P, 2 * DP, P]) for j in range(2)]
        h0 = [sbuf(p1, f"h0_{l}", [P, TT, D]) for l in NL]
        wb = pt[:, 0].rearrange("p (o d) -> p o d", d=DP)
        h = [sbuf(p1, f"h{l}", [P, TT, D]) for l in NL]
        hT = [sbuf(p1, f"hT{l}", [P, KC, T + 1]) for l in NL]
        s = [sbuf(p1, f"s{l}", [P, TT, D]) for l in NL]
        w12 = [sbuf(p1, f"w12_{l}", [P, 4, T]) for l in NL]
        wT0 = w12[0][:].rearrange("p a n -> p (a n)")[:, 0:SETUP_MATS * KC * D].rearrange(
            "p (m c n) -> p m c n", m=SETUP_MATS, c=KC)
        probs = [pt[:, j].rearrange("p (a n) -> p a n", a=2) for j in range(2)] + [hT[l][:, :, 1:T + 1] for l in NL]
        w3 = [sbuf(p1, f"w3_{l}", [P, KC, T]) for l in NL]
        stats = [sbuf(p1, f"stats{l}", [P, TT, 6]) for l in NL]
        mv = [sbuf(p1, f"mv{l}", [P, TT, 2]) for l in NL]
        ve = [sbuf(p1, f"ve{l}", [P, TT]) for l in NL]
        rstd = [sbuf(p1, f"rstd{l}", [P, TT]) for l in NL]
        qkhi = pt[:].rearrange("p a (b n) -> p (a b) n", b=2).bitcast(F32R)
        qklo = sbuf(p1, "qklo", [P, 4, T], F32R)
        qst = sbuf(p1, "qst", [P, GROUPS, 2, T], F32R)
        kst = sbuf(p1, "kst", [P, GROUPS, 4, T], F32R)
        vp = [sbuf(p1, f"vp{l}", [P, TT, H, 2 * HD]) for l in NL]
        mx = sbuf(p1, "mx", [P, 2, TT, 4])
        mparts = sbuf(p1, "mparts", [P, 2, TT, 2, 4], F32R)
        mhl = qklo[0:8, 0, :]
        gl = [sbuf(p1, f"gl{l}", [P, 6, TT, E]) for l in NL]
        gm = [sbuf(p1, f"gm{l}", [P, 4, TT]) for l in NL]
        top8 = [sbuf(p1, f"top8{l}", [P, TT, 8]) for l in NL]
        idx8 = [sbuf(p1, f"idx8{l}", [P, TT, 8], U32) for l in NL]
        idxf = [sbuf(p1, f"idxf{l}", [P, TT, 2]) for l in NL]
        slot_i = [sbuf(p1, f"slot_i{l}", [P, TT, 2], I32) for l in NL]

        def by_token(ap):
            return ap.rearrange("p a n -> p (a n)").rearrange("p (t d) -> p t d", t=TT)

        def flat(ap):
            return ap.rearrange("p a n -> p (a n)")

        xr, xk = [w12[l][:, 0:2] for l in NL], [w12[l][:, 2:4] for l in NL]
        num = [s[l][:].rearrange("p t d -> p (t d)").rearrange("p (g q) -> p g q", g=2) for l in NL]
        ao = [w12[l][:, 0:2].rearrange("p a n -> p (a n)").rearrange("p (t d) -> p t d", t=TT) for l in NL]
        aoT = [w12[l][:, 2:4] for l in NL]
        rden = [sbuf(p1, f"rden{l}", [P, TT, 4]) for l in NL]
        G = [w12[l][:, 0:2, 0:D] for l in NL]
        GV = [w3[l][:, :, 0:D] for l in NL]
        BM = [w12[l][:, 2:4, 0:D] for l in NL]

        w_loaded = sem("weights_loaded")
        pool_setup, dve_setup, act_setup = sem("pool_setup"), sem("dve_setup"), sem("act_setup")
        dve_own = sem("dve_own")
        x_loaded, x_used = sems("x_loaded", TT), sems("x_used", TT)
        h_ready = [sems(f"h_ready{l}_", 5) for l in NL]
        var_ready, rstd_ready = sems("var_ready"), sems("rstd_ready")
        mix_ready = sems("mix_ready")
        relu_sq, at_ready = sems("relu_squared"), sems("at_ready")
        a2_ready, a2_capped, sq_ready = sems("a2_ready"), sems("a2_capped"), sems("sqrt_ready")
        sT_ready = sems("scan_ready")
        h3_stored, x1_stored = sems("h3_stored"), sems("x1_stored")
        qkb_ready, swapped, qk_ready = sems("qk_biased"), sems("qk_swapped"), sems("qk_turned")
        hi_ready, lo_ready = sem("hi_ready"), sem("lo_ready")
        parts_stored, v_ready = sems("parts_stored"), sems("v_ready")
        st_loaded, st_used = sems("stack_loaded", GROUPS), sems("stack_used", GROUPS)
        av_copied, bo_added = sems("av_copied"), sems("bo_added")
        mparts_ready, mhl_ready, mx_stored = sem("mx_parts_ready"), sem("mx_rows_ready"), sem("mx_stored")
        mx_loaded = sems("mx_loaded", GROUPS)
        ao_ready = sems("ao_ready")
        gate_in, gate_exp, mask_ready = sems("gate_in"), sems("gate_exp"), sems("mask_ready")
        slot_ready, scattered, rows_away = sems("slot_ready"), sems("scattered"), sems("rows_away")
        settled, settled_pool, settled_sp = sem("settled"), sem("settled_pool"), sem("settled_sp")

        block = p1.enter_context(nc.Block())

        def mat(n):
            return MATS.index(n)

        def rows(ap):
            return ap.rearrange("(c p) n -> p c n", p=P)

        def bcast(ap, n):
            return ap.rearrange("(o n) -> o n", o=1).broadcast_to([P, n])

        LOADS = []
        for n, name in zip(MATS, ("L0_tok_weighted_sum", "L0_attn_w_q", "L0_attn_w_k", "L0_ffn_W_r",
                                  "L0_ffn_W_k", "L0_ffn_W_v", "L1_attn_Wi", "L1_attn_Wr")):
            LOADS.append((wnat[:, mat(n)], rows(a[name])))
        LOADS += [(wv0[:], rows(a["L0_attn_w_v"])), (wqk[:, :, 0:D], rows(a["L1_ffn_Wq"])),
                  (wqk[:, :, D:2 * D], rows(a["L1_ffn_Wk"])), (wv1[:], rows(a["L1_ffn_Wv"])),
                  (wg[:], rows(a["L1_ffn_Wg"])), (wo[:], rows(a["L1_ffn_Wo"])), (bo[:], bcast(a["L1_ffn_bo"], D)),
                  (wb[:].rearrange("p o d -> p (o d)"), bcast(a["L0_tok_weight"].rearrange("o d -> (o d)"), D * DP)),
                  (bqk[:, 0:D], bcast(a["L1_ffn_bq"], D)), (bqk[:, D:2 * D], bcast(a["L1_ffn_bk"], D)),
                  (bv[:], bcast(a["L1_ffn_bv"], D)), (bg[:], bcast(a["L1_ffn_bg"], E)),
                  (g1t[:], bcast(a["L1_ffn_g1"], D)), (be1t[:], bcast(a["L1_ffn_be1"], D)),
                  (cap[:, 0:1], bcast(a["L1_attn_cap_lambda"], 1)),
                  (rope[:], a["rope"].rearrange("c (t p) d -> p c t d", p=P))]
        for j, name in enumerate(("L0_ffn_mu_r", "L0_ffn_mu_k", "L1_attn_bi", "L1_attn_br")):
            LOADS.append((cols[:, j, :], a[name].rearrange("(c p) -> p c", p=P)))

        x_src = a["x"].rearrange("b (t p) i d -> b t p (i d)", p=P)

        @block.sync
        def _(sp):
            with nc.allow_non_contiguous_dma(reason="columns and broadcasts of small weights, once"):
                for dst, src in LOADS:
                    sp.dma_start(dst, src).then_inc(w_loaded, 16)
            full(sp, ("at",), None)

            def load_x(batch, tiles=range(TT)):
                for tt in tiles:
                    sp.wait_ge(x_used[tt], batch + 1)
                    sp.sem_inc(settled_sp, 1)
                    sp.dma_start(xin[:, tt, :], x_src[bass.ds(batch, 1), tt].rearrange("o p n -> (o p) n")
                                 ).then_inc(x_loaded[tt], 16)

            for l in NL:
                load_x(l)

            def turn(i, last):
                if not last:
                    load_x((i + 1) * LANES)
                for l in NL:
                    sp.wait_ge(h_ready[l][3], i + 1)
                    sp.dma_start(h3_all.rearrange("(b t p) d -> b p t d", t=TT, p=P)[bass.ds(i * LANES + l, 1)].rearrange("o p t d -> (o p) t d"),
                                 h[l][:]).then_inc(h3_stored[l], 16)
                def store_parts(l):
                    sp.wait_ge(hi_ready, 4 * i + 2 * l + 2)
                    sp.dma_start(qk_parts[l, 0].rearrange("(c p) t -> p c t", p=P), qkhi.bitcast(F32)).then_inc(parts_stored[l], 16)
                    sp.wait_ge(lo_ready, 4 * i + 2 * l + 2)
                    sp.dma_start(qk_parts[l, 1].rearrange("(c p) t -> p c t", p=P), qklo[:].bitcast(F32)).then_inc(parts_stored[l], 16)

                def load_stacks(l, g, n):
                    if g == 0:
                        sp.wait_ge(parts_stored[l], 32 * i + 32)
                        sp.sem_inc(settled_sp, 1)
                    for at in range(g, g + n):
                        sp.wait_ge(st_used[at], i * LANES + l + 1)
                    for e in range(2):
                        for part in range(PARTS):
                            p0 = 64 * e + HD * part
                            for st, base, kinds in ((qst[:], 0, (0, 1, 0)), (kst[:, :, e:4:2, :], 1, (0, 0, 1))):
                                src = qk_parts[l, kinds[part]].rearrange("(q g e d) t -> q e d g t", q=2, e=2, d=HD)[base, e, :, 2 * g:2 * (g + n)]
                                dst = st[p0:p0 + HD, g:g + n]
                                sp.dma_start(dst.bitcast(F32), src.rearrange("d (g j) t -> d g j t", g=n)).then_inc(st_loaded[g], 16)
                        p0 = 64 * e + ROW_MAX
                        sp.dma_start(qst[p0:p0 + 2, g:g + n].bitcast(F32), kst[64:66, g:g + n, 0:4:2, :].bitcast(F32)).then_inc(st_loaded[g], 16)

                groups = [(l, g) for l in NL for g in range(GROUPS)]
                store_parts(0)
                load_stacks(0, 0, 1)
                store_parts(1)
                if not last:
                    load_x((i + 1) * LANES + 1, range(TT - 1))
                load_stacks(0, 1, GROUPS - 1)
                if not last:
                    load_x((i + 1) * LANES + 1, [TT - 1])
                for at, (l, g) in enumerate(groups):
                    n = i * LANES * GROUPS + at
                    sp.wait_ge(mhl_ready, n + 1)
                    sp.dma_start(mx_parts[l, g].rearrange("k h t -> (k h) t"), mhl.bitcast(F32)).then_inc(mx_stored, 16)
                    sp.wait_ge(mx_stored, n * 16 + 32)
                    for e in range(2):
                        src = mx_parts[l, g].rearrange("k (j e) t -> e k j t", e=2)[e]
                        p0 = 64 * e + ROW_MAX
                        sp.dma_start(qst[p0:p0 + 2, g].bitcast(F32), src).then_inc(mx_loaded[g], 16)
                    if 2 <= at < GROUPS + 2:
                        load_stacks(*groups[at + 2], 1)
                for l in NL:
                    sp.wait_ge(h_ready[l][4], i + 1)
                    sp.dma_start(x1_all.rearrange("(b t p) d -> b p t d", t=TT, p=P)[bass.ds(i * LANES + l, 1)].rearrange("o p t d -> (o p) t d"),
                                 h[l][:]).then_inc(x1_stored[l], 16)

            with sp.Fori(0, ITERS - 1) as i:
                turn(i, False)
            turn(ITERS - 1, True)
            for l in NL:
                sp.wait_ge(h3_stored[l], 16 * ITERS)
                sp.wait_ge(x1_stored[l], 16 * (ITERS + 1))
        @block.tensor
        def _(pe):
            mm, tr = nc.tensor.matmul, nc.tensor.transpose
            pe.wait_ge(pool_setup, 2)
            pe.wait_ge(w_loaded, 16 * N_LOADS)
            for m in MATS:
                g = room(pe, ("wT", m), None)
                for kc in range(KC):
                    for c in range(KC):
                        ins = tr(g[:, kc, c * P:(c + 1) * P], wnat[:, mat(m), c, kc * P:(kc + 1) * P], ident[:])
                ins.then_inc(fill_sem(("wT", m), None), 1)
            for m in ("wq", "wk"):
                copied(pe, ("wT", m), None)
            g = room(pe, ("at",), None)
            for kc in range(KC):
                for dc in range(KC):
                    ins = mm(g[:, 0, kc * D:(kc + 1) * D], wT0[:, mat("wk"), dc, kc * P:(kc + 1) * P],
                             wT0[:, mat("wq"), dc, :], start=dc == 0, stop=dc == KC - 1)
            ins.then_inc(fill_sem(("at",), None), 1)
            pe.wait_ge(dve_setup, 3)

            def mix_tokens(key, i):
                kind, l, tt = key
                j = (l * TT + tt) % 2
                if kind == "xT":
                    batch = l if i is None else (i + 1) * LANES + l
                    pe.wait_ge(x_loaded[tt], 16 * (batch + 1))
                    g = flat(room(pe, key, i)).rearrange("p (k t) -> p k t", t=P)
                    xv = xin[:, tt].rearrange("p (c q d) -> p d c q", c=2, d=DP)
                    for k in range(2 * DP):
                        ins = tr(g[:, k, :], xv[:, k // 2, k % 2, :], ident[:])
                    ins.then_inc(fill_sem(key, i), 1)
                else:
                    copied(pe, ("xT", l, tt), i)
                    g = room(pe, key, i)
                    for k in range(2 * DP):
                        ins = mm(g[:, 0, 0:D], xT[j][:, k, :], wc[:, k, :], start=k == 0, stop=k == 2 * DP - 1)
                        if k == 0:
                            ins.then_inc(x_used[tt], 1)
                    ins.then_inc(fill_sem(key, i), 1)

            for key in mixing_order():
                mix_tokens(key, None)

            def turn(i, last):
                def to_channels(stage, l, src):
                    g = room(pe, (stage, l), i)
                    for dc in range(KC):
                        for tt in range(TT):
                            ins = tr(g[:, dc, tt * P:(tt + 1) * P], src[:, tt, dc * P:(dc + 1) * P], ident[:])
                    ins.then_inc(fill_sem((stage, l), i), 1)

                def by_tokens(stage, l, lhs, rhs, n=D):
                    g = flat(room(pe, (stage, l), i))
                    chunks = rhs.shape[1]
                    for tt in range(TT):
                        for kc in range(chunks):
                            ins = mm(g[:, tt * n:(tt + 1) * n], lhs[:, kc, tt * P:(tt + 1) * P], rhs[:, kc, :],
                                     start=kc == 0, stop=kc == chunks - 1)
                    ins.then_inc(fill_sem((stage, l), i), 1)

                def by_channels(stage, l, wt, rhs):
                    g = room(pe, (stage, l), i)
                    for dc in range(KC):
                        for kc in range(KC):
                            ins = mm(g[:, dc, :], wt[:, kc, dc * P:(dc + 1) * P], rhs[:, kc, :],
                                     start=kc == 0, stop=kc == KC - 1)
                    ins.then_inc(fill_sem((stage, l), i), 1)

                def square(stage, l, lhs, rhs, chunks):
                    g = room(pe, (stage, l), i)
                    for dc in range(KC):
                        for kc in range(chunks):
                            ins = mm(g[:, 0, dc * D:(dc + 1) * D], lhs[:, kc, dc * P:(dc + 1) * P], rhs[:, kc, :],
                                     start=kc == 0, stop=kc == chunks - 1)
                    ins.then_inc(fill_sem((stage, l), i), 1)

                for l in NL:
                    pe.wait_ge(h_ready[l][0], TT * (i + 1))
                    to_channels("hT0", l, h0[l])
                for l in NL:
                    square("g", l, h0[l], h0[l], TT)
                for l in NL:
                    copied(pe, ("g", l), i)
                    square("gv", l, G[l], wv0, KC)
                for l in NL:
                    copied(pe, ("gv", l), i)
                    square("b", l, at16, GV[l], KC)
                for l in NL:
                    copied(pe, ("b", l), i)
                    by_tokens("y", l, hT[l][:, :, 1:T + 1], BM[l])

                for l in NL:
                    pe.wait_ge(h_ready[l][1], i + 1)
                    to_channels("hT1", l, h[l])
                for l in NL:
                    pe.wait_ge(mix_ready[l], 2 * i + 1)
                    by_tokens("r", l, xr[l], wT[:, mat("fr") - SETUP_MATS])
                for l in NL:
                    pe.wait_ge(mix_ready[l], 2 * i + 2)
                    by_channels("k", l, wT[:, mat("fk") - SETUP_MATS], xk[l])
                for l in NL:
                    pe.wait_ge(relu_sq[l], i + 1)
                    by_tokens("kv", l, s[l][:].rearrange("p t d -> p (t d)").rearrange("p (c n) -> p c n", c=KC), wT[:, mat("fv") - SETUP_MATS])

                for l in NL:
                    pe.wait_ge(h_ready[l][2], i + 1)
                    to_channels("hT2", l, h[l])
                for l in NL:
                    copied(pe, ("hT2", l), i)
                    by_channels("rt", l, wT[:, mat("ar") - SETUP_MATS], hT[l][:, :, 1:T + 1])
                for l in NL:
                    by_channels("it", l, wT[:, mat("ai") - SETUP_MATS], hT[l][:, :, 1:T + 1])
                for l in NL:
                    pe.wait_ge(sT_ready[l], i + 1)
                    g = flat(room(pe, ("back", l), i))
                    for tt in range(TT):
                        for dc in range(KC):
                            ins = tr(g[:, tt * D + dc * P:tt * D + (dc + 1) * P], w3[l][:, dc, tt * P:(tt + 1) * P], ident[:])
                    ins.then_inc(fill_sem(("back", l), i), 1)

                for l in NL:
                    pe.wait_ge(h_ready[l][3], i + 1)
                    to_channels("hT3", l, h[l])
                for half_ in range(2):
                    for l in NL:
                        copied(pe, ("hT3", l), i)
                        g = room(pe, (f"qk{half_}", l), i)
                        for tb in range(2):
                            tt = 2 * half_ + tb
                            for kc in range(KC):
                                ins = mm(g[:, tb, :], hT[l][:, kc, 1 + tt * P:1 + (tt + 1) * P], wqk[:, kc, :],
                                         start=kc == 0, stop=kc == KC - 1)
                        ins.then_inc(fill_sem((f"qk{half_}", l), i), 1)
                for l in NL:
                    by_tokens("v", l, hT[l][:, :, 1:T + 1], wv1)
                before, attention, after = attention_order(last)
                for l in NL:
                    for key in before[l]:
                        mix_tokens(key, i)
                    for half_ in range(2):
                        pe.wait_ge(qk_ready[l], i + 1)
                        g = room(pe, (f"qkT{half_}", l), i)
                        for c in range(2):
                            for tt in range(TT):
                                c0 = (2 * half_ + c) * P
                                ins = tr(g[:, c, tt * P:(tt + 1) * P], w12[l][:, tt, c0:c0 + P], ident[:])
                        ins.then_inc(fill_sem((f"qkT{half_}", l), i), 1)

                def values(l, g, kt):
                    copied(pe, ("exp", l, g, 2 * kt + 1), i)
                    av = granule(slot_of(("av", l, g), i))
                    if kt == 0:
                        room(pe, ("av", l, g), i)
                        pe.wait_ge(v_ready[l], i + 1)
                    for j in range(4):
                        ins = mm(av[32 * j:32 * j + 32, :], vp[l][:, kt, 4 * g + j, :], probs[(2 * kt + j // 2) % 4][:, j % 2, :],
                                 start=kt == 0, stop=kt == TT - 1)
                    if kt == TT - 1:
                        ins.then_inc(fill_sem(("av", l, g), i), 1)
                        pe.sem_inc(st_used[g], 1)

                late = []
                def mix_ahead(stage):
                    for key in after.get(stage, ()):
                        mix_tokens(key, i)

                third = [key for key in list(plan_of(i)) if slot_of(key, i) == SLOTS - 1]
                for key in before[LANES]:
                    mix_tokens(key, i)
                later = ("aoT", "wo", "xT1", "gate", "rank")
                copied(pe, [key for key in third if key[0] not in later and key not in sum(after.values(), [])][-1], i)
                for key in attention:
                    kind, l, g = key[:3]
                    if kind in ("xT", "tok"):
                        mix_tokens(key, i)
                    elif kind == "max":
                        if key[3] == 0:
                            which, value = stacks_value(l, g, i)
                            pe.wait_ge(st_loaded[which], value)
                        j, qt = key[3] // TT, key[3] % TT
                        out_ = room(pe, key, i)
                        mm(out_, qst[:, g, j // 2, qt * P:(qt + 1) * P], kst[:, g, j, :], start=True, stop=True
                           ).then_inc(fill_sem(key, i), 1)
                    elif kind == "exp":
                        n = key[3]
                        if n == 0:
                            pe.wait_ge(mx_loaded[g], (i * LANES + l + 1) * 32)
                        kt, pair = n // 2, n % 2
                        out_ = room(pe, key, i)
                        for e in range(2):
                            ins = mm(out_[:, e, :], kst[:, g, 2 * pair + e, kt * P:(kt + 1) * P], qst[:, g, pair, :],
                                     start=True, stop=True)
                        ins.then_inc(fill_sem(key, i), 1)
                        if n % 2 == 1:
                            late.append((l, g, kt))
                            if len(late) > 1:
                                values(*late.pop(0))
                    elif kind == "maxT":
                        pe.wait_ge(mparts_ready, (i * LANES + l) * GROUPS + g + 1)
                        out_ = room(pe, key, i)
                        for tt in range(TT):
                            ins = tr(out_[0:8, tt * P:(tt + 1) * P],
                                     mparts[:, g % 2, tt].rearrange("p k h -> p (k h)").bitcast(F32), ident[:])
                        ins.then_inc(fill_sem(key, i), 1)
                    elif kind == "avT":
                        pe.wait_ge(av_copied[l], GROUPS * i + g + 1)
                        out_ = room(pe, key, i)
                        for tt in range(TT):
                            ins = tr(out_[:, tt * P:(tt + 1) * P], num[l][:, g % 2, tt * P:(tt + 1) * P], ident[:])
                        ins.then_inc(fill_sem(key, i), 1)
                    elif (l, g) == (LANES - 1, GROUPS - 1):
                        while late:
                            values(*late.pop(0))

                for n in (14, 15):
                    copied(pe, ("max", LANES - 1, GROUPS - 1, n), i)

                for l in NL:
                    pe.wait_ge(ao_ready[l], GROUPS * (i + 1))
                    to_channels("aoT", l, ao[l])
                for l in NL:
                    copied(pe, ("aoT", l), i)
                    by_tokens("wo", l, aoT[l], wo)
                mix_ahead("xT1")
                for l in NL:
                    pe.wait_ge(h_ready[l][4], i + 1)
                    to_channels("xT1", l, h[l])
                mix_ahead("gate")
                for l in NL:
                    copied(pe, ("xT1", l), i)
                    by_tokens("gate", l, hT[l][:, :, 1:T + 1], wg, n=E)
                mix_ahead("rank")
                for l in NL:
                    pe.wait_ge(mask_ready[l], i + 1)
                    g = flat(room(pe, ("rank", l), i))
                    mask = gl[l][:, 2].rearrange("p t e -> p (t e)")
                    mm(g[:, 0:TT * E], ntri[:], mask, start=True, stop=True)
                    mm(g[:, TT * E:2 * TT * E], ones[:], mask, start=True, stop=True
                       ).then_inc(fill_sem(("rank", l), i), 1)

            with pe.Fori(0, ITERS - 1) as i:
                turn(i, False)
            turn(ITERS - 1, True)

        @block.scalar
        def _(act):
            fn = nc.scalar.activation
            act.wait_ge(dve_setup, 2)
            fn(cap[:, 2:3], cap[:, 1:2], ACT.Exp, scale=-1.0).then_inc(act_setup, 1)
            act.wait_ge(act_setup, 1)
            fn(cap[:, 3:4], cap[:, 2:3], ACT.Ln, bias=1.0).then_inc(act_setup, 1)
            act.wait_ge(dve_setup, 3)

            def copy_mixed(key, i):
                kind, l, tt = key
                src = full(act, key, i)
                if kind == "xT":
                    fn(xT[(l * TT + tt) % 2][:], flat(src).rearrange("p (k t) -> p k t", t=P), ACT.Copy
                       ).then_inc(drain_sem(key, i), 1)
                else:
                    fn(h0[l][:, tt, :], src[:, 0, 0:D], ACT.Copy).then_inc(drain_sem(key, i), 1)
                    copied(act, key, i)
                    act.sem_inc(h_ready[l][0], 1)

            for key in mixing_order():
                copy_mixed(key, None)

            def turn(i, last):
                def copy_out(key, dst):
                    src = full(act, key, i)
                    fn(dst, src, ACT.Copy).then_inc(drain_sem(key, i), 1)

                for l in NL:
                    copy_out(("hT0", l), hT[l][:, :, 1:T + 1])
                for l in NL:
                    src = full(act, ("gv", l), i)[:, 0].rearrange("p (c n) -> p c n", c=KC)
                    fn(GV[l], src, ACT.Copy).then_inc(drain_sem(("gv", l), i), 1)
                for l in NL:
                    copy_out(("hT1", l), hT[l][:, :, 1:T + 1])
                for l in NL:
                    src = full(act, ("r", l), i)
                    fn(w3[l][:], src, ACT.Sigmoid).then_inc(drain_sem(("r", l), i), 1)
                for l in NL:
                    src = full(act, ("k", l), i)
                    ka = s[l][:].rearrange("p t d -> p (t d)").rearrange("p (c n) -> p c n", c=KC)
                    fn(ka, src, ACT.Relu).then_inc(drain_sem(("k", l), i), 1)
                    copied(act, ("k", l), i)
                    fn(ka, ka, ACT.Square).then_inc(relu_sq[l], 1)
                for l in NL:
                    copy_out(("hT2", l), hT[l][:, :, 1:T + 1])
                def gate_sigmoid(stage, l, j, dst):
                    src = full(act, (stage, l), i)
                    for dc in range(KC):
                        ins = fn(w12[l][:, dst + dc, :], src[:, dc, :], ACT.Sigmoid, bias=cols[:, j, dc:dc + 1])
                    ins.then_inc(drain_sem((stage, l), i), 1)

                for l in NL:
                    gate_sigmoid("rt", l, 3, 2)
                for l in NL:
                    copied(act, ("rt", l), i)
                    fn(w3[l][:], xk[l], ACT.Exp, scale=cap[:, 7:8]).then_inc(a2_ready[l], 1)
                    act.wait_ge(a2_ready[l], i + 1)
                    fn(xk[l], xk[l], ACT.Exp, scale=cap[:, 4:5]).then_inc(at_ready[l], 1)
                for l in NL:
                    act.wait_ge(a2_capped[l], i + 1)
                    fn(w3[l][:], w3[l][:], ACT.Sqrt, scale=-1.0, bias=1.0).then_inc(sq_ready[l], 1)
                for l in NL:
                    gate_sigmoid("it", l, 2, 0)
                for l in NL:
                    copy_out(("hT3", l), hT[l][:, :, 1:T + 1])
                before, attention, after = attention_order(last)
                for l in NL:
                    for key in before[l]:
                        copy_mixed(key, i)
                    for half_ in range(2):
                        src = full(act, (f"qkT{half_}", l), i)
                        if l == 1 and half_ == 0:
                            act.wait_ge(parts_stored[0], 32 * i + 32)
                        fn(qkhi[:, 2 * half_:2 * half_ + 2, :], src, ACT.Copy).then_inc(hi_ready, 1)
                for key in before[LANES]:
                    copy_mixed(key, i)
                n = 0
                for key in attention:
                    if key[0] in ("xT", "tok"):
                        copy_mixed(key, i)
                    elif key[0] == "exp":
                        src = full(act, key, i)
                        fn(probs[n % 4], src, ACT.Exp, scale=HD ** -0.5).then_inc(drain_sem(key, i), 1)
                        n += 1
                    elif key[0] == "maxT":
                        _, l, g = key
                        gn = (i * LANES + l) * GROUPS + g
                        act.wait_ge(mx_stored, 16 * gn + 16)
                        fn(mhl, full(act, key, i)[0:8, :], ACT.Copy).then_inc(drain_sem(key, i), 1)
                        copied(act, key, i)
                        act.sem_inc(mhl_ready, 1)
                    elif key[0] == "av":
                        _, l, g = key
                        full(act, key, i)
                        fn(num[l][:, g % 2, :], granule(slot_of(key, i)), ACT.Copy).then_inc(drain_sem(key, i), 1)
                        copied(act, key, i)
                        act.sem_inc(av_copied[l], 1)
                for l in NL:
                    copy_out(("aoT", l), aoT[l])
                for key in after.get("xT1", ()):
                    copy_mixed(key, i)
                for l in NL:
                    copy_out(("xT1", l), hT[l][:, :, 1:T + 1])
                for key in after.get("gate", ()):
                    copy_mixed(key, i)
                for l in NL:
                    act.wait_ge(gate_in[l], i + 1)
                    fn(gl[l][:, 1], gl[l][:, 0], ACT.Exp).then_inc(gate_exp[l], 1)
                for key in after.get("rank", ()):
                    copy_mixed(key, i)

            with act.Fori(0, ITERS - 1) as i:
                turn(i, False)
            turn(ITERS - 1, True)

        @block.vector
        def _(dve):
            v = nc.vector
            setup = Count(dve_own)
            dve.sem_inc(dve_setup, 1)
            for l in NL:
                v.memset(hT[l][:, :, 0:1], 0.0)
                v.memset(vp[l][:], 1.0)
            v.memset(qst[:].bitcast(F32), 0.0)
            for e in range(2):
                v.memset(kst[64 * e:64 * e + 64, :, e:4:2, :].bitcast(F32), 1.0)
                v.memset(kst[64 * e:64 * e + 64, :, 1 - e:4:2, :].bitcast(F32), 0.0)
            v.memset(ones[:], 1.0)
            v.memset(half[:], -0.5)
            setup.link(dve, v.memset(run[:], 0.0))
            dve.wait_ge(w_loaded, 16 * N_LOADS)
            setup.link(dve, v.tensor_scalar(cap[:, 5:6], cap[:, 0:1], -1.0, None, ALU.mult))
            v.tensor_tensor(cap[:, 1:2], cap[:, 0:1], cap[:, 5:6], ALU.max).then_inc(dve_setup, 1)
            setup.link(dve, v.tensor_scalar(ncols[:, 0:2], cols[:, 0:2], -1.0, 1.0, ALU.mult, ALU.add))
            for m in MATS:
                src = full(dve, ("wT", m), None)[:, :, 0:D]
                dst = wT0[:, mat(m)] if mat(m) < SETUP_MATS else wT[:, mat(m) - SETUP_MATS]
                v.tensor_copy(dst, src).then_inc(drain_sem(("wT", m), None), 1)
            copied(dve, ("wT", MATS[-1]), None)
            for k in range(2 * DP):
                setup.link(dve, v.tensor_tensor(wc[:, k, :], wT0[:, mat("ws"), k % 2, :], wb[:, :, k // 2], ALU.mult))
            src = full(dve, ("at",), None)[:, 0].rearrange("p (c n) -> p c n", c=KC)
            v.tensor_scalar(at16[:], src, D ** 0.5, None, ALU.mult).then_inc(drain_sem(("at",), None), 1)
            copied(dve, ("at",), None)
            dve.wait_ge(act_setup, 2)
            setup.link(dve, v.tensor_scalar(cap[:, 5:6], cap[:, 0:1], 0.0, None, ALU.max))
            setup.link(dve, v.tensor_tensor(cap[:, 6:7], cap[:, 5:6], cap[:, 3:4], ALU.add))
            v.tensor_scalar(cap[:, 7:8], cap[:, 6:7], -16.0, None, ALU.mult)
            v.tensor_scalar(cap[:, 4:5], cap[:, 6:7], -8.0, None, ALU.mult).then_inc(dve_setup, 1)

            def turn(i, last):
                own = Count(dve_own, i * DVE_LINKS + setup.n)

                def link(ins):
                    own.link(dve, ins)

                def moments(l, src):
                    for tt in range(TT):
                        ins = v.bn_stats(stats[l][:, tt, :], src[:, tt, :])
                    link(ins)
                    dve.sem_inc(settled, 1)
                    for tt in range(TT):
                        ins = v.bn_aggr(mv[l][:, tt, :], stats[l][:, tt, :])
                    link(ins)
                    v.tensor_scalar(ve[l][:], mv[l][:, :, 1], EPS, None, ALU.add).then_inc(var_ready[l], 1)

                def normalise(l, src, n, dst):
                    dve.wait_ge(rstd_ready[l], NORMS * i + n + 1)
                    for tt in range(TT):
                        ins = v.tensor_scalar(dst[:, tt, :], src[:, tt, :], mv[l][:, tt, 0:1], rstd[l][:, tt:tt + 1],
                                              ALU.subtract, ALU.mult)
                    return ins

                for l in NL:
                    src = full(dve, ("g", l), i)[:, 0].rearrange("p (c n) -> p c n", c=KC)
                    v.tensor_copy(G[l], src).then_inc(drain_sem(("g", l), i), 1)
                for l in NL:
                    src = full(dve, ("b", l), i)[:, 0].rearrange("p (c n) -> p c n", c=KC)
                    v.tensor_copy(BM[l], src).then_inc(drain_sem(("b", l), i), 1)
                for l in NL:
                    src = by_token(full(dve, ("y", l), i))
                    dve.wait_ge(h_ready[l][0], TT * (i + 1))
                    v.tensor_tensor(s[l][:], src, h0[l][:], ALU.add).then_inc(drain_sem(("y", l), i), 1)
                    copied(dve, ("y", l), i)
                    moments(l, s[l])
                for l in NL:
                    dve.wait_ge(x1_stored[l], 16 * i + 16)
                    dve.wait_ge(rows_away[l], i + 1)
                    normalise(l, s[l], 0, h[l]).then_inc(h_ready[l][1], 1)

                for l in NL:
                    copied(dve, ("hT1", l), i)
                    for j, dst in ((0, xr[l]), (1, xk[l])):
                        for dc in range(KC):
                            ins = v.tensor_scalar(dst[:, dc, :], hT[l][:, dc, 1:T + 1], cols[:, j, dc:dc + 1], None, ALU.mult)
                        link(ins)
                        for dc in range(KC):
                            ins = v.scalar_tensor_tensor(out=dst[:, dc, :], in0=hT[l][:, dc, 0:T],
                                                         scalar=ncols[:, j, dc:dc + 1], in1=dst[:, dc, :],
                                                         op0=ALU.mult, op1=ALU.add)
                        ins.then_inc(mix_ready[l], 1)
                for l in NL:
                    copied(dve, ("r", l), i)
                    src = by_token(full(dve, ("kv", l), i))
                    v.tensor_tensor(s[l][:], src, by_token(w3[l]), ALU.mult).then_inc(drain_sem(("kv", l), i), 1)
                    copied(dve, ("kv", l), i)
                    dve.wait_ge(h_ready[l][1], i + 1)
                    link(v.tensor_tensor(s[l][:], s[l][:], h[l][:], ALU.add))
                    moments(l, s[l])
                for l in NL:
                    normalise(l, s[l], 1, h[l]).then_inc(h_ready[l][2], 1)

                for l in NL:
                    dve.wait_ge(a2_ready[l], i + 1)
                    v.tensor_scalar(w3[l][:], w3[l][:], 1.0, None, ALU.min).then_inc(a2_capped[l], 1)
                for l in NL:
                    dve.wait_ge(sq_ready[l], i + 1)
                    copied(dve, ("hT2", l), i)
                    link(v.tensor_tensor(w3[l][:], w3[l][:], hT[l][:, :, 1:T + 1], ALU.mult))
                for l in NL:
                    copied(dve, ("it", l), i)
                    dve.wait_ge(at_ready[l], i + 1)
                    link(v.tensor_tensor(xr[l], xr[l], w3[l][:], ALU.mult))
                    for dc in range(KC):
                        ins = v.tensor_tensor_scan(w3[l][:, dc, :], xk[l][:, dc, :], xr[l][:, dc, :], 0.0, ALU.mult, ALU.add)
                    link(ins)
                    v.tensor_tensor(w3[l][:], w3[l][:], hT[l][:, :, 1:T + 1], ALU.add).then_inc(sT_ready[l], 1)
                for l in NL:
                    src = by_token(full(dve, ("back", l), i))
                    moments(l, src)
                for l in NL:
                    ins = normalise(l, by_token(granule(slot_of(("back", l), i))), 2, h[l])
                    link(ins)
                    dve.sem_inc(drain_sem(("back", l), i), 1)
                    dve.sem_inc(h_ready[l][3], 1)

                for half_ in range(2):
                    for l in NL:
                        src = full(dve, (f"qk{half_}", l), i)
                        v.tensor_tensor(w12[l][:, 2 * half_:2 * half_ + 2, :], src,
                                        bqk[:].unsqueeze(1).to_broadcast([P, 2, 2 * D]), ALU.add
                                        ).then_inc(drain_sem((f"qk{half_}", l), i), 1)
                        copied(dve, (f"qk{half_}", l), i)
                        if half_ == 1:
                            dve.sem_inc(qkb_ready[l], 1)
                for l in NL:
                    src = by_token(full(dve, ("v", l), i)).rearrange("p t (h d) -> p t h d", d=HD)
                    bias = bv[:].rearrange("p (h d) -> p h d", d=HD).unsqueeze(1).to_broadcast([P, TT, H, HD])
                    link(v.tensor_tensor(vp[l][:, :, :, 0:HD], src, bias, ALU.add))
                    dve.sem_inc(drain_sem(("v", l), i), 1)
                    dve.sem_inc(v_ready[l], 1)
                for l in NL:
                    dve.wait_ge(swapped[l], i + 1)
                    qk = w12[l][:].rearrange("p t (h d) -> p t h d", d=HD)
                    cos = rope[:, 0].unsqueeze(2).to_broadcast([P, TT, 2 * H, HD])
                    link(v.tensor_tensor(qk, qk, cos, ALU.mult))
                    v.tensor_tensor(w12[l][:, 0:2, :], w12[l][:, 0:2, :], w3[l][:], ALU.add)
                    v.tensor_tensor(w12[l][:, 2:4, :], w12[l][:, 2:4, :],
                                    s[l][:].rearrange("p t d -> p (t d)").rearrange("p (a n) -> p a n", a=2), ALU.add
                                    ).then_inc(qk_ready[l], 1)
                for l in NL:
                    for half_ in range(2):
                        src = full(dve, (f"qkT{half_}", l), i)
                        c0 = 2 * half_
                        if l == 1 and half_ == 0:
                            dve.wait_ge(parts_stored[0], 32 * i + 32)
                        dve.wait_ge(hi_ready, 4 * i + 2 * l + half_ + 1)
                        link(v.tensor_tensor(qklo[:, c0:c0 + 2, :], src, qkhi[:, c0:c0 + 2, :].bitcast(F32), ALU.subtract))
                        dve.sem_inc(drain_sem((f"qkT{half_}", l), i), 1)
                        dve.sem_inc(lo_ready, 1)

                for key in attention_order(last)[1]:
                    kind, l, g = key[:3]
                    if kind == "max":
                        head, qt = key[3] // TT, key[3] % TT
                        src = full(dve, key, i)
                        v.tensor_reduce(mx[:, g % 2, qt, head:head + 1], src, AX_X, ALU.max
                                        ).then_inc(drain_sem(key, i), 1)
                        if key[3] == 15:
                            copied(dve, key, i)
                            copied(dve, ("max", l, g, 14), i)
                            hi, lo = mparts[:, g % 2, :, 0, :], mparts[:, g % 2, :, 1, :]
                            link(v.tensor_scalar(hi, mx[:, g % 2], -1.0, None, ALU.mult))
                            v.scalar_tensor_tensor(out=lo, in0=mx[:, g % 2], scalar=-1.0, in1=hi.bitcast(F32),
                                                   op0=ALU.mult, op1=ALU.subtract).then_inc(mparts_ready, 1)
                    elif kind == "avT":
                        src = full(dve, key, i).rearrange("p (t h c) -> p t h c", t=TT, h=4)
                        link(v.reciprocal(rden[l][:], src[:, :, :, HD]))
                        v.tensor_tensor(ao[l].rearrange("p t (h d) -> p t h d", d=HD)[:, :, 4 * g:4 * g + 4, :], src[:, :, :, 0:HD],
                                        rden[l][:].unsqueeze(3).to_broadcast([P, TT, 4, HD]), ALU.mult
                                        ).then_inc(drain_sem(key, i), 1)
                        copied(dve, key, i)
                        dve.sem_inc(ao_ready[l], 1)
                for l in NL:
                    src = by_token(full(dve, ("wo", l), i))
                    dve.wait_ge(bo_added[l], i + 1)
                    v.tensor_tensor(s[l][:], src, h[l][:], ALU.add).then_inc(drain_sem(("wo", l), i), 1)
                    copied(dve, ("wo", l), i)
                    moments(l, s[l])
                for l in NL:
                    link(normalise(l, s[l], 3, s[l]))
                    link(v.tensor_tensor(s[l][:], s[l][:], g1t[:].unsqueeze(1).to_broadcast([P, TT, D]), ALU.mult))
                    dve.wait_ge(h3_stored[l], 16 * (i + 1))
                    v.tensor_tensor(h[l][:], s[l][:], be1t[:].unsqueeze(1).to_broadcast([P, TT, D]), ALU.add
                                    ).then_inc(h_ready[l][4], 1)

                for l in NL:
                    src = flat(full(dve, ("gate", l), i))[:, 0:TT * E].rearrange("p (t e) -> p t e", e=E)
                    lg = gl[l][:, 0]

                    def wide(ap):
                        return ap.unsqueeze(2).to_broadcast([P, TT, E])

                    v.tensor_tensor(lg, src, bg[:].unsqueeze(1).to_broadcast([P, TT, E]), ALU.add
                                    ).then_inc(drain_sem(("gate", l), i), 1)
                    copied(dve, ("gate", l), i)
                    link(v.tensor_reduce(gm[l][:, 0, :], lg, AX_X, ALU.max))
                    v.tensor_tensor(lg, lg, wide(gm[l][:, 0, :]), ALU.subtract).then_inc(gate_in[l], 1)
                for l in NL:
                    ex = gl[l][:, 1]
                    dve.wait_ge(gate_exp[l], i + 1)
                    link(v.tensor_reduce(gm[l][:, 1, :], ex, AX_X, ALU.add))
                    link(v.reciprocal(gm[l][:, 1, :], gm[l][:, 1, :]))
                    link(v.tensor_tensor(ex, ex, wide(gm[l][:, 1, :]), ALU.mult))
                    dve.sem_inc(settled, 1)
                    for tt in range(TT):
                        ins = v.max(top8[l][:, tt, :], ex[:, tt, :])
                    link(ins)
                    dve.sem_inc(settled, 1)
                    for tt in range(TT):
                        ins = v.max_index(idx8[l][:, tt, :], top8[l][:, tt, :], ex[:, tt, :])
                    link(ins)
                    link(v.tensor_tensor(gm[l][:, 2, :], top8[l][:, :, 0], top8[l][:, :, 1], ALU.add))
                    link(v.reciprocal(gm[l][:, 2, :], gm[l][:, 2, :]))
                    v.tensor_tensor(topw_all[:, bass.ds((i * LANES + l) * TT, TT), :], top8[l][:, :, 0:2],
                                    gm[l][:, 2, :].unsqueeze(2).to_broadcast([P, TT, 2]), ALU.mult)
                    link(v.tensor_copy(idxf[l][:], idx8[l][:, :, 0:2]))
                    for k in range(2):
                        ins = v.tensor_tensor(gl[l][:, 3 + k], iota8[:].unsqueeze(1).to_broadcast([P, TT, E]),
                                              wide(idxf[l][:, :, k]), ALU.is_equal)
                    link(ins)
                    v.tensor_tensor(gl[l][:, 2], gl[l][:, 3], gl[l][:, 4], ALU.add).then_inc(mask_ready[l], 1)
                for l in NL:
                    src = flat(full(dve, ("rank", l), i))
                    ranks = src[:, 0:TT * E].rearrange("p (t e) -> p t e", e=E)
                    totals = src[:, TT * E:2 * TT * E].rearrange("p (t e) -> p t e", e=E)
                    base = gl[l][:, 5]
                    link(v.tensor_tensor(base[:, 0, :], run[:], region[:], ALU.add))
                    for tt in range(1, TT):
                        link(v.tensor_tensor(base[:, tt, :], base[:, tt - 1, :], totals[:, tt - 1, :], ALU.add))
                    for tt in range(TT):
                        link(v.tensor_tensor(run[:], run[:], totals[:, tt, :], ALU.add))
                    link(v.tensor_tensor(base, base, ranks, ALU.add))
                    dve.sem_inc(drain_sem(("rank", l), i), 1)
                    for k in range(2):
                        link(v.tensor_tensor(gl[l][:, 3 + k], gl[l][:, 3 + k], base, ALU.mult))
                        link(v.tensor_reduce(gm[l][:, 2 + k, :], gl[l][:, 3 + k], AX_X, ALU.add))
                    dve.wait_ge(rows_away[l], i + 1)
                    for k in range(2):
                        v.tensor_copy(slot_i[l][:, :, k], gm[l][:, 2 + k, :])
                        ins = v.tensor_copy(slots_all[:, bass.ds((i * LANES + l) * TT, TT), k], gm[l][:, 2 + k, :])
                    link(ins)
                    dve.sem_inc(slot_ready[l], 1)
                assert own.n == DVE_LINKS, own.n

            with dve.Fori(0, ITERS - 1) as i:
                turn(i, False)
            turn(ITERS - 1, True)

        @block.gpsimd
        def _(pool):
            q = nc.gpsimd
            q.memset(ident[:], 0.0).then_inc(pool_setup, 1)
            pool.wait_ge(pool_setup, 1)
            q.affine_select(out=ident[:], in_=ident[:], compare_op=ALU.not_equal, fill=1.0, base=0,
                            pattern=[[-1, P]], channel_multiplier=1).then_inc(pool_setup, 1)
            q.memset(ntri[:], 1.0).then_inc(pool_setup, 1)
            pool.wait_ge(pool_setup, 3)
            q.affine_select(out=ntri[:], in_=ntri[:], compare_op=ALU.is_gt, fill=0.0, base=0,
                            pattern=[[1, P]], channel_multiplier=-1)
            q.iota(iota8[:], pattern=[[1, E]], base=0, channel_multiplier=0, allow_small_or_imprecise_dtypes=True)
            q.iota(region[:], pattern=[[REGION, E]], base=0, channel_multiplier=0,
                   allow_small_or_imprecise_dtypes=True).then_inc(pool_setup, 1)
            for sem_ in drained + x_used + rows_away + st_used:
                pool.sem_inc(sem_, 1)
            for sem_ in x1_stored + [mx_stored]:
                pool.sem_inc(sem_, 16)
            pool.wait_ge(dve_own, 1)
            pool.wait_ge(w_loaded, 16 * N_LOADS)

            def turn(i, last):
                def rsqrt(n):
                    for l in NL:
                        pool.wait_ge(var_ready[l], NORMS * i + n + 1)
                        q.tensor_tensor(rstd[l][:], ve[l][:], half[:], ALU.pow).then_inc(rstd_ready[l], 1)

                for n in range(3):
                    rsqrt(n)
                for l in NL:
                    pool.wait_ge(qkb_ready[l], i + 1)
                    for tt in range(TT):
                        x_ = w12[l][:, tt, :].rearrange("p (h d) -> p h d", d=HD)
                        y_ = (w3[l][:, tt, :] if tt < 2 else
                              s[l][:].rearrange("p t d -> p (t d)")[:, (tt - 2) * T:(tt - 1) * T]).rearrange("p (h d) -> p h d", d=HD)
                        for half_ in range(2):
                            a_, b_ = half_ * HD // 2, (1 - half_) * HD // 2
                            sin = rope[:, 1, tt, a_:a_ + HD // 2].unsqueeze(1).to_broadcast([P, 2 * H, HD // 2])
                            ins = q.tensor_tensor(y_[:, :, a_:a_ + HD // 2], x_[:, :, b_:b_ + HD // 2], sin, ALU.mult)
                    ins.then_inc(swapped[l], 1)
                for l in NL:
                    pool.wait_ge(h3_stored[l], 16 * (i + 1))
                    full(pool, ("hT3", l), i)
                    q.tensor_tensor(h[l][:], h[l][:], bo[:].unsqueeze(1).to_broadcast([P, TT, D]), ALU.add).then_inc(bo_added[l], 1)
                rsqrt(3)
                for l in NL:
                    pool.wait_ge(slot_ready[l], i + 1)
                    pool.sem_inc(settled_pool, 1)
                    for tt in range(TT):
                        for k in range(2):
                            q.indirect_dma_start(xs[:], bass.IndirectOffsetOnAxis(ap=slot_i[l][:, tt, k:k + 1], axis=0),
                                                 h[l][:, tt, :], None).then_inc(scattered[l], 16)
                for l in NL:
                    pool.wait_ge(scattered[l], 16 * 2 * TT * (i + 1))
                    pool.sem_inc(rows_away[l], 1)

            with pool.Fori(0, ITERS - 1) as i:
                turn(i, False)
            turn(ITERS - 1, True)
        p1.close()

        NJ = range(2)
        p2 = ctx.enter_context(ExitStack())
        w1 = sbuf(p2, "w1", [P, E, KC, FF])
        w2 = sbuf(p2, "w2", [P, E, FC, D])
        b1 = sbuf(p2, "b1", [P, E, FF])
        b2 = sbuf(p2, "b2", [P, E, D])
        zeros = sbuf(p2, "zeros", [P, D])
        steps = sbuf(p2, "steps", [P, STEPS, 2], I32)
        ends = sbuf(p2, "ends", [P, 2, E])
        pad = sbuf(p2, "pad", [P, E], I32)
        many = sbuf(p2, "many", [P, E, B * T // P])
        edge = sbuf(p2, "edge", [P, B * T // P])
        step_no = sbuf(p2, "step_no", [P, STEPS])
        past = sbuf(p2, "past", [P, STEPS, E])
        tmp = sbuf(p2, "tmp", [P, 4, STEPS])
        first = sbuf(p2, "first", [P, E])
        pad_f = sbuf(p2, "pad_f", [P, E])
        slot_f = sbuf(p2, "slot_f", [P, 2 * TILES])
        spare = sbuf(p2, "spare", [P, E - 1])
        beyond = sbuf(p2, "beyond", [P, 2 * TILES, E - 1])
        moved = sbuf(p2, "moved", [P, 2 * TILES])
        xrow = [sbuf(p2, f"xrow{j}", [P, D]) for j in NJ]
        xTe = [sbuf(p2, f"xTe{j}", [P, KC, P]) for j in NJ]
        he = [sbuf(p2, f"he{j}", [P, FF]) for j in NJ]
        heT = [sbuf(p2, f"heT{j}", [P, FC, P]) for j in NJ]
        ye = [sbuf(p2, f"ye{j}", [P, D]) for j in NJ]

        table_ready, setup2 = sem("steps_ready"), sem("phase2_setup")
        experts_loaded, padded = sem("experts_loaded"), sem("padded")
        rows_loaded, rows_turned, rowsT_ready = sems("rows_loaded", 2), sem("rows_turned"), sem("rowsT_ready")
        l1_done, l1_biased, gelu_done = sem("l1_done"), sem("l1_biased"), sem("gelu_done")
        h_turned, hT_act, hT_dve = sem("hidden_turned"), sem("hiddenT_act"), sem("hiddenT_dve")
        l2_done, l2_biased, y_stored = sem("l2_done"), sem("l2_biased"), sems("y_stored", 2)
        own2, zeros_ready, first_loaded = sem("dve_own2"), sem("zeros_ready"), sem("first_expert_loaded")

        def at_least(eng, sem_, value):
            if not isinstance(value, int) or value > 0:
                eng.wait_ge(sem_, value)

        def pipeline(eng, lag, body):
            for n in range(4):
                body(n, n % 2)
            with eng.Fori(0, (STEPS - 6) // 2) as it:
                for j in NJ:
                    body(it * 2 + 4 + j, j)
            for n in range(STEPS - 2, STEPS + lag):
                body(n, n % 2)

        def inside(n, lag):
            return not isinstance(n, int) or 0 <= n - lag < STEPS

        blk = ctx.enter_context(ExitStack())
        block2 = blk.enter_context(nc.Block())
        pX = ps[:, 0, 0:KC * P]
        pY = ps[:, 1, 0:D]
        pH = [ps[:, 2:4, :], ps[:, 4:6, :]]
        pT = ps[:, 6:8, :]

        @block2.sync
        def _(sp):
            sp.dma_start(w1[:, 0], rows(a["L1_ffn_W1"][0])).then_inc(first_loaded, 16)
            sp.dma_start(w2[:, 0], rows(a["L1_ffn_W2"][0])).then_inc(first_loaded, 16)
            sp.wait_ge(zeros_ready, 1)
            sp.dma_start(xs[E * REGION:ROWS].rearrange("(e p) d -> p e d", p=P),
                         zeros[:].unsqueeze(1).to_broadcast([P, E, D])).then_inc(padded, 16)
            sp.wait_ge(table_ready, 1)
            for e in range(E):
                row = sp.value_load(pad[0:1, e:e + 1], min_val=0, max_val=ROWS - P)
                sp.dma_start(xs[bass.ds(row, P), :], zeros[:]).then_inc(padded, 16)
            sp.wait_ge(padded, 16 * (E + 1))

            def body(n, j):
                if inside(n, 0):
                    row = sp.value_load(steps[0:1, bass.ds(n, 1), 1], min_val=0, max_val=ROWS - P)
                    at_least(sp, rows_turned, n - 1)
                    sp.dma_start(xrow[j][:], xs[bass.ds(row, P), :]).then_inc(rows_loaded[j], 16)
                if inside(n, 4):
                    sp.wait_ge(l2_biased, n - 3)
                    sp.dma_start(ys.rearrange("(s p) d -> s p d", p=P)[bass.ds(n - 4, 1)].rearrange("o p d -> (o p) d"), ye[j][:]).then_inc(y_stored[j], 16)

            pipeline(sp, 4, body)
            for j in NJ:
                sp.wait_ge(y_stored[j], 16 * STEPS // 2)

        @block2.tensor
        def _(pe):
            mm, tr = nc.tensor.matmul, nc.tensor.transpose
            pe.wait_ge(first_loaded, 32)
            pe.wait_ge(table_ready, 1)

            def turn_rows(n, j):
                pe.wait_ge(rows_loaded[j], 16 * ((n - j) // 2 + 1) if isinstance(n, int) else 8 * (n - j) + 16)
                at_least(pe, rowsT_ready, n)
                for kc in range(KC):
                    ins = tr(pX[:, kc * P:(kc + 1) * P], xrow[j][:, kc * P:(kc + 1) * P], ident[:])
                ins.then_inc(rows_turned, 1)

            def body(n, j):
                if isinstance(n, int) and n == 0:
                    turn_rows(0, 0)
                if inside(n, 0):
                    e = pe.value_load(steps[0:1, bass.ds(n, 1), 0], min_val=0, max_val=E - 1)
                    pe.wait_ge(rowsT_ready, n + 1)
                    at_least(pe, l1_biased, n - 1)
                    pe.wait_ge(experts_loaded, e * 64 + 32)
                    for c in range(2):
                        for kc in range(KC):
                            ins = mm(pH[j][:, c, :], xTe[j][:, kc, :],
                                     w1[:, bass.ds(e, 1), kc, c * 512:(c + 1) * 512].rearrange("p o n -> p (o n)"),
                                     start=kc == 0, stop=kc == KC - 1)
                    ins.then_inc(l1_done, 1)
                if inside(n, -1):
                    turn_rows(n + 1, 1 - j)
                if inside(n, 1):
                    pe.wait_ge(gelu_done, n)
                    at_least(pe, hT_act, n - 1)
                    at_least(pe, hT_dve, n - 1)
                    for f in range(FC):
                        ins = tr(pT[:, f // 4, (f % 4) * P:(f % 4 + 1) * P], he[1 - j][:, f * P:(f + 1) * P], ident[:])
                    ins.then_inc(h_turned, 1)
                if inside(n, 2):
                    e = pe.value_load(steps[0:1, bass.ds(n - 2, 1), 0], min_val=0, max_val=E - 1)
                    pe.wait_ge(hT_act, n - 1)
                    pe.wait_ge(hT_dve, n - 1)
                    at_least(pe, l2_biased, n - 2)
                    for f in range(FC):
                        ins = mm(pY, heT[j][:, f, :],
                                 w2[:, bass.ds(e, 1), f, :].rearrange("p o n -> p (o n)"),
                                 start=f == 0, stop=f == FC - 1)
                    ins.then_inc(l2_done, 1)

            pipeline(pe, 2, body)

        @block2.scalar
        def _(act):
            fn = nc.scalar.activation

            def turned(n, j):
                act.wait_ge(rows_turned, n + 1)
                at_least(act, l1_done, n - 1)
                fn(xTe[j][:], pX.rearrange("p (c t) -> p c t", c=KC), ACT.Copy).then_inc(rowsT_ready, 1)

            def body(n, j):
                if isinstance(n, int) and n == 0:
                    turned(0, 0)
                if inside(n, -1):
                    turned(n + 1, 1 - j)
                if inside(n, 1):
                    act.wait_ge(h_turned, n)
                    at_least(act, l2_done, n - 2)
                    fn(heT[1 - j][:, 0:4, :], pT[:, 0, :].rearrange("p (f t) -> p f t", t=P), ACT.Copy).then_inc(hT_act, 1)
                if inside(n, 0):
                    act.wait_ge(l1_biased, n + 1)
                    fn(he[j][:], he[j][:], ACT.Gelu).then_inc(gelu_done, 1)

            pipeline(act, 1, body)

        @block2.vector
        def _(dve):
            v = nc.vector
            own = Count(own2)

            def link(ins):
                own.link(dve, ins)

            v.memset(zeros[:], 0.0).then_inc(zeros_ready, 1)
            dve.wait_ge(setup2, 1)
            counts = run[:].unsqueeze(2).to_broadcast([P, E, B * T // P])
            link(v.tensor_tensor(many[:], counts, edge[:].unsqueeze(1).to_broadcast([P, E, B * T // P]), ALU.is_gt))
            link(v.tensor_reduce(ends[:, 0, :], many[:], AX_X, ALU.add))
            link(v.tensor_copy(ends[:, 1, 0:1], ends[:, 0, 0:1]))
            for e in range(1, E):
                link(v.tensor_tensor(ends[:, 1, e:e + 1], ends[:, 1, e - 1:e], ends[:, 0, e:e + 1], ALU.add))
            link(v.tensor_tensor(past[:], step_no[:].unsqueeze(2).to_broadcast([P, STEPS, E]),
                                 ends[:, 1, :].unsqueeze(1).to_broadcast([P, STEPS, E]), ALU.is_ge))
            link(v.tensor_reduce(tmp[:, 0, :], past[:], AX_X, ALU.add))
            link(v.tensor_tensor(past[:], past[:], ends[:, 0, :].unsqueeze(1).to_broadcast([P, STEPS, E]), ALU.mult))
            link(v.tensor_reduce(tmp[:, 1, :], past[:], AX_X, ALU.add))
            link(v.tensor_tensor(tmp[:, 1, :], step_no[:], tmp[:, 1, :], ALU.subtract))
            link(v.tensor_scalar(tmp[:, 1, :], tmp[:, 1, :], float(P), None, ALU.mult))
            link(v.tensor_scalar(tmp[:, 2, :], tmp[:, 0, :], float(REGION), None, ALU.mult))
            link(v.tensor_tensor(tmp[:, 1, :], tmp[:, 1, :], tmp[:, 2, :], ALU.add))
            link(v.tensor_scalar(tmp[:, 0, :], tmp[:, 0, :], float(E - 1), None, ALU.min))
            v.tensor_copy(steps[:, :, 0], tmp[:, 0, :])
            v.tensor_copy(steps[:, :, 1], tmp[:, 1, :])
            link(v.tensor_tensor(pad_f[:], first[:], run[:], ALU.add))
            v.tensor_copy(pad[:], pad_f[:]).then_inc(table_ready, 1)
            dve.wait_ge(table_ready, 1)
            link(v.tensor_scalar(spare[:], ends[:, 0, 0:E - 1], float(P), float(-REGION), ALU.mult, ALU.add))
            link(v.tensor_copy(slot_f[:], flat(slots_all[:])))
            link(v.tensor_tensor(beyond[:], slot_f[:].unsqueeze(2).to_broadcast([P, 2 * TILES, E - 1]),
                                 first[:, 1:E].unsqueeze(1).to_broadcast([P, 2 * TILES, E - 1]), ALU.is_ge))
            link(v.tensor_tensor(beyond[:], beyond[:], spare[:].unsqueeze(1).to_broadcast([P, 2 * TILES, E - 1]), ALU.mult))
            link(v.tensor_reduce(moved[:], beyond[:], AX_X, ALU.add))
            link(v.tensor_tensor(slot_f[:], slot_f[:], moved[:], ALU.add))
            link(v.tensor_copy(flat(slots_all[:]), slot_f[:]))

            def body(n, j):
                if inside(n, 0):
                    e = dve.value_load(steps[0:1, bass.ds(n, 1), 0], min_val=0, max_val=E - 1)
                    dve.wait_ge(l1_done, n + 1)
                    at_least(dve, h_turned, n - 1)
                    v.tensor_tensor(he[j][:], pH[j].rearrange("p a n -> p (a n)"),
                                    b1[:, bass.ds(e, 1), :].rearrange("p o n -> p (o n)"), ALU.add).then_inc(l1_biased, 1)
                if inside(n, 1):
                    dve.wait_ge(h_turned, n)
                    at_least(dve, l2_done, n - 2)
                    v.tensor_copy(heT[1 - j][:, 4:8, :], pT[:, 1, :].rearrange("p (f t) -> p f t", t=P)).then_inc(hT_dve, 1)
                if inside(n, 2):
                    e = dve.value_load(steps[0:1, bass.ds(n - 2, 1), 0], min_val=0, max_val=E - 1)
                    dve.wait_ge(l2_done, n - 1)
                    at_least(dve, y_stored[j], 16 * ((n - 2) // 2) if isinstance(n, int) else 8 * (n - j) - 16)
                    v.tensor_tensor(ye[j][:], pY, b2[:, bass.ds(e, 1), :].rearrange("p o n -> p (o n)"),
                                    ALU.add).then_inc(l2_biased, 1)

            pipeline(dve, 2, body)

        @block2.gpsimd
        def _(pool):
            q = nc.gpsimd
            q.iota(edge[:], pattern=[[P, B * T // P]], base=0, channel_multiplier=0, allow_small_or_imprecise_dtypes=True)
            q.iota(step_no[:], pattern=[[1, STEPS]], base=0, channel_multiplier=0, allow_small_or_imprecise_dtypes=True)
            q.iota(first[:], pattern=[[REGION, E]], base=0, channel_multiplier=0,
                   allow_small_or_imprecise_dtypes=True).then_inc(setup2, 1)
            for e in range(E):
                if e > 0:
                    q.dma_start(w1[:, e], rows(a["L1_ffn_W1"][e])).then_inc(experts_loaded, 16)
                    q.dma_start(w2[:, e], rows(a["L1_ffn_W2"][e])).then_inc(experts_loaded, 16)
                q.dma_start(b1[:, e], bcast(a["L1_ffn_b1"][e], FF)).then_inc(experts_loaded, 16)
                q.dma_start(b2[:, e], bcast(a["L1_ffn_b2"][e], D)).then_inc(experts_loaded, 16)
                pool.wait_ge(experts_loaded, 64 * e + 32)

        blk.close()
        p2.close()

        NG = range(4)
        GRP = TILES // 2 // len(NG)
        g2t = sbuf(ctx, "g2t", [P, D])
        be2t = sbuf(ctx, "be2t", [P, D])
        x1b = [sbuf(ctx, f"x1b{j}", [P, 2, D]) for j in NG]
        h3b = [sbuf(ctx, f"h3b{j}", [P, 2, D]) for j in NG]
        yb = [sbuf(ctx, f"yb{j}", [P, 2, 2, D]) for j in NG]
        ob = [sbuf(ctx, f"ob{j}", [P, 2, D]) for j in NG]
        where = [sbuf(ctx, f"where{j}", [P, 2, 2], I32) for j in NG]
        stats3 = [sbuf(ctx, f"stats3_{j}", [P, 2, 6]) for j in NG]
        mv3 = [sbuf(ctx, f"mv3_{j}", [P, 2, 2]) for j in NG]
        ve3 = [sbuf(ctx, f"ve3_{j}", [P, 2]) for j in NG]
        rstd3 = [sbuf(ctx, f"rstd3_{j}", [P, 2]) for j in NG]
        gains_loaded, where_ready = sem("gains_loaded"), sem("where_ready")
        x1b_loaded, h3b_loaded, yb_loaded = sems("x1b_loaded", len(NG)), sems("h3b_loaded", len(NG)), sems("yb_loaded", len(NG))
        rows_added, h3_added = sem("rows_added"), sem("h3_added")
        y_weighted, h3_biased = sem("y_weighted"), sem("h3_biased")
        var3, sd3_ready = sem("var3_ready"), sem("deviation3_ready")
        out_ready, out_stored, own3, settled3 = sem("out_ready"), sems("out_stored", len(NG)), sem("dve_own3"), sem("settled3")
        settled_p3 = sem("settled_pool3")

        blk = ctx.enter_context(ExitStack())
        block3 = blk.enter_context(nc.Block())

        def nth(i, j, n=0, of=1):
            return (i * of + n) * len(NG) + j + 1

        tiled = lambda ap: ap.rearrange("(t p) d -> t p d", p=P)
        out_t = out.rearrange("b (t p) d -> (b t) p d", p=P)

        @block3.sync
        def _(sp):
            sp.dma_start(g2t[:], bcast(a["L1_ffn_g2"], D)).then_inc(gains_loaded, 16)
            sp.dma_start(be2t[:], bcast(a["L1_ffn_be2"], D)).then_inc(gains_loaded, 16)

            def load(i, j, used):
                t0 = (i * len(NG) + j) * 2
                if used is not None:
                    sp.wait_ge(rows_added, nth(used, j))
                sp.dma_start(x1b[j][:], tiled(x1_all)[bass.ds(t0, 2)].rearrange("t p d -> p t d")).then_inc(x1b_loaded[j], 16)
                if used is not None:
                    sp.wait_ge(h3_added, nth(used, j))
                sp.dma_start(h3b[j][:], tiled(h3_all)[bass.ds(t0, 2)].rearrange("t p d -> p t d")).then_inc(h3b_loaded[j], 16)

            def turn(i, last):
                for j in NG:
                    if not last:
                        load(i + 1, j, i)
                for j in NG:
                    t0 = (i * len(NG) + j) * 2
                    sp.wait_ge(out_ready, nth(i, j))
                    sp.dma_start(out_t[bass.ds(t0, 2)].rearrange("t p d -> p t d"), ob[j][:]).then_inc(out_stored[j], 16)

            for j in NG:
                load(0, j, None)
            with sp.Fori(0, GRP - 1) as i:
                turn(i, False)
            turn(GRP - 1, True)
            for j in NG:
                sp.wait_ge(out_stored[j], 16 * (GRP + 1))

        @block3.gpsimd
        def _(pool):
            q = nc.gpsimd
            for sem_ in out_stored:
                pool.sem_inc(sem_, 16)
            pool.wait_ge(gains_loaded, 32)

            def gather(i, j, used):
                if used is not None:
                    pool.wait_ge(rows_added, nth(used, j))
                pool.sem_inc(settled_p3, 1)
                q.tensor_copy(where[j][:], slots_all[:, bass.ds((i * len(NG) + j) * 2, 2), :]).then_inc(where_ready, 1)
                pool.wait_ge(where_ready, nth(i, j))
                pool.sem_inc(settled_p3, 1)
                for t in range(2):
                    for k in range(2):
                        q.indirect_dma_start(yb[j][:, t, k, :], None, ys[:],
                                             bass.IndirectOffsetOnAxis(ap=where[j][:, t, k:k + 1], axis=0)).then_inc(yb_loaded[j], 16)

            def turn(i, last):
                for j in NG:
                    pool.wait_ge(h3b_loaded[j], 16 * i + 16)
                    q.tensor_tensor(h3b[j][:], h3b[j][:], be2t[:].unsqueeze(1).to_broadcast([P, 2, D]), ALU.add
                                    ).then_inc(h3_biased, 1)
                for j in NG:
                    if not last:
                        gather(i + 1, j, i)

            for j in NG:
                gather(0, j, None)
            with pool.Fori(0, GRP - 1) as i:
                turn(i, False)
            turn(GRP - 1, True)

        @block3.scalar
        def _(act):
            with act.Fori(0, GRP) as i:
                for j in NG:
                    act.wait_ge(yb_loaded[j], 64 * i + 64)
                    for t in range(2):
                        for k in range(2):
                            ins = nc.scalar.activation(yb[j][:, t, k, :], yb[j][:, t, k, :], ACT.Copy,
                                                       scale=topw_all[:, bass.ds((i * len(NG) + j) * 2 + t, 1), k])
                    ins.then_inc(y_weighted, 1)
                for n in range(2):
                    for j in NG:
                        act.wait_ge(var3, nth(i, j, n, 2))
                        nc.scalar.activation(ve3[j][:], ve3[j][:], ACT.Sqrt).then_inc(sd3_ready, 1)

        @block3.vector
        def _(dve):
            v = nc.vector
            dve.wait_ge(gains_loaded, 32)
            with dve.Fori(0, GRP) as i:
                own = Count(own3, i * LINKS3)

                def link(ins):
                    own.link(dve, ins)

                def moments(j):
                    for t in range(2):
                        ins = v.bn_stats(stats3[j][:, t, :], ob[j][:, t, :])
                    link(ins)
                    dve.sem_inc(settled3, 1)
                    for t in range(2):
                        ins = v.bn_aggr(mv3[j][:, t, :], stats3[j][:, t, :])
                    link(ins)
                    v.tensor_scalar(ve3[j][:], mv3[j][:, :, 1], EPS, None, ALU.add).then_inc(var3, 1)

                def normalise(j, n):
                    dve.wait_ge(sd3_ready, nth(i, j, n, 2))
                    link(v.reciprocal(rstd3[j][:], ve3[j][:]))
                    for t in range(2):
                        ins = v.tensor_scalar(ob[j][:, t, :], ob[j][:, t, :], mv3[j][:, t, 0:1], rstd3[j][:, t:t + 1],
                                              ALU.subtract, ALU.mult)
                    return ins

                for j in NG:
                    dve.wait_ge(x1b_loaded[j], 16 * i + 16)
                    dve.wait_ge(y_weighted, nth(i, j))
                    dve.wait_ge(out_stored[j], 16 * i + 16)
                    link(v.tensor_tensor(ob[j][:], yb[j][:, :, 0, :], yb[j][:, :, 1, :], ALU.add))
                    v.tensor_tensor(ob[j][:], ob[j][:], x1b[j][:], ALU.add).then_inc(rows_added, 1)
                    dve.wait_ge(rows_added, nth(i, j))
                    moments(j)
                for j in NG:
                    link(normalise(j, 0))
                    link(v.tensor_tensor(ob[j][:], ob[j][:], g2t[:].unsqueeze(1).to_broadcast([P, 2, D]), ALU.mult))
                    dve.wait_ge(h3_biased, nth(i, j))
                    v.tensor_tensor(ob[j][:], ob[j][:], h3b[j][:], ALU.add).then_inc(h3_added, 1)
                    dve.wait_ge(h3_added, nth(i, j))
                    moments(j)
                for j in NG:
                    normalise(j, 1).then_inc(out_ready, 1)
                assert own.n == LINKS3, own.n

        blk.close()


_INS = ["x", "L0_tok_weight", "L0_tok_weighted_sum", "L0_attn_w_q", "L0_attn_w_k", "L0_attn_w_v", "L0_ffn_W_r",
        "L0_ffn_W_k", "L0_ffn_W_v", "L0_ffn_mu_r", "L0_ffn_mu_k", "L1_attn_Wi", "L1_attn_bi", "L1_attn_Wr",
        "L1_attn_br", "L1_attn_cap_lambda", "L1_ffn_Wq", "L1_ffn_bq", "L1_ffn_Wk", "L1_ffn_bk", "L1_ffn_Wv",
        "L1_ffn_bv", "L1_ffn_Wo", "L1_ffn_bo", "L1_ffn_Wg", "L1_ffn_bg", "L1_ffn_W1", "L1_ffn_b1", "L1_ffn_W2",
        "L1_ffn_b2", "L1_ffn_g1", "L1_ffn_be1", "L1_ffn_g2", "L1_ffn_be2"]


def rope_table():
    import numpy as np

    inv = (np.float32(1.0) / np.float32(10000.0) ** (np.arange(0, HD, 2, dtype=np.float32) / np.float32(HD))).astype(np.float32)
    freqs = np.arange(T, dtype=np.float32)[:, None] * inv[None, :]
    cos, sin = np.cos(freqs), np.sin(freqs)
    return np.stack([np.concatenate([cos, cos], 1), np.concatenate([-sin, sin], 1)]).astype(np.float32)


def kernel(**inputs):
    import numpy as _np
    import concourse.bacc as _bacc
    from concourse import mybir as _mybir
    from concourse.bass_utils import run_bass_kernel_spmd as _run

    nc = _bacc.Bacc("TRN2", target_bir_lowering=False, num_devices=1)
    arrays, args = {}, {}
    for name in _INS + ["rope"]:
        a = rope_table() if name == "rope" else _np.ascontiguousarray(inputs[name])
        arrays[f"in_{name}_dram"] = a
        args[name] = nc.dram_tensor(f"in_{name}_dram", a.shape, _mybir.dt.from_np(a.dtype), kind="ExternalInput").ap()
    out = nc.dram_tensor("out_0_dram", (B, T, D), F32, kind="ExternalOutput").ap()
    tower(nc, args, out)
    r = _run(nc, [arrays], core_ids=[0])
    return r.results[0]["out_0_dram"]
```
